# Optimizing a Trainium2 kernel written in Bass

```python
import numpy as np
import jax
import jax.numpy as jnp

def _softmax(x, axis=-1):
    return jax.nn.softmax(x, axis=axis)

def _gelu(x):
    return jax.nn.gelu(x, approximate=True)

def _silu(x):
    return jax.nn.silu(x)

def _sigmoid(x):
    return jax.nn.sigmoid(x)

def _layernorm(x, axis=-1, eps=1e-05):
    m = jnp.mean(x, axis=axis, keepdims=True)
    v = jnp.var(x, axis=axis, keepdims=True)
    return (x - m) / jnp.sqrt(v + eps)

def _scatter_add(tgt, idx, src, axis=0):
    return tgt.at[idx].add(src)

def _segment_sum(src, seg, n):
    return jax.ops.segment_sum(src, seg, n)
kernel_name = 'mk_perceiver_d2_seqx_r8_e969d4'

def setup_inputs(seed: int=0):
    np.random.seed(seed)
    _w = jnp.asarray

    def _rec_inputs():
        import jax
        import jax.numpy as jnp
        _rk = jax.random.key(seed)
        x = -0.0002928 + 1 * jax.random.normal(jax.random.fold_in(_rk, 1), (16, 64, 256), jnp.float32)
        _lenS = 64 - jax.random.randint(jax.random.fold_in(_rk, 7), (16,), 0, max(1, 64 // 4) + 1, jnp.int32)
        _lenS2 = 128 - jax.random.randint(jax.random.fold_in(_rk, 8), (16,), 0, max(1, 128 // 4) + 1, jnp.int32)
        _ctx_512P = jax.random.normal(jax.random.fold_in(_rk, 11), (16, 16, 64), jnp.float32)
        _ctx_512c = jax.random.dirichlet(jax.random.fold_in(_rk, 511), 0.3 * jnp.ones((16,), jnp.float32), (16, 128))
        _ctx_512t = jnp.einsum('bsk,bkd->bsd', _ctx_512c, _ctx_512P)
        _ctx_512t = _ctx_512t * jax.lax.rsqrt(jnp.mean(jnp.square(_ctx_512t)) + 1e-12) * 0.953939
        ctx_512 = 0.000227908 + 0.99994 * (_ctx_512t + 0.3 * jax.random.normal(jax.random.fold_in(_rk, 611), (16, 128, 64), jnp.float32))
        return (x, ctx_512)
    x, ctx_512 = _rec_inputs()

    def _L0_xattn_setup():
        import jax, jax.numpy as jnp
        import numpy as np
        B, S, L = (2, 128, 128)
        DIM_Q, H, K, D_C, D_CQ, R = (256, 16, 128, 64, 192, 64)

        def _rope_tables(length, dim):
            inv = 1.0 / 10000.0 ** (jnp.arange(0, dim, 2, dtype=jnp.float32) / dim)
            f = jnp.arange(length, dtype=jnp.float32)[:, None] * inv[None, :]
            sin = jnp.repeat(jnp.sin(f), 2, axis=-1)
            cos = jnp.repeat(jnp.cos(f), 2, axis=-1)
            return (sin, cos)

        def _rotate_half(x):
            half = x.shape[-1] // 2
            return jnp.concatenate([-x[..., half:], x[..., :half]], axis=-1)

        def _apply_rope(x, sin, cos):
            return x * cos + _rotate_half(x) * sin
        key = jax.random.key(seed)
        ks = jax.random.split(key, 8)
        return {'hidden_q': jax.random.normal(ks[0], (B, S, DIM_Q), jnp.float32), 'kv_c': jax.random.normal(ks[1], (B, L, D_C), jnp.float32), 'Wq': jax.random.normal(ks[2], (H * K, DIM_Q), jnp.float32) / np.sqrt(DIM_Q).astype(np.float32), 'w_kc_q': jax.random.normal(ks[3], (H, K, D_CQ), jnp.float32) / np.sqrt(K).astype(np.float32), 'w_kc_kv': jax.random.normal(ks[4], (H, K, D_C), jnp.float32) / np.sqrt(K).astype(np.float32), 'W_qr': jax.random.normal(ks[5], (H, D_CQ, R), jnp.float32) / np.float32(np.sqrt(D_CQ) * np.sqrt(R)), 'W_kr': jax.random.normal(ks[6], (H, D_C, R), jnp.float32) / np.sqrt(D_C).astype(np.float32), 'Wo': jax.random.normal(ks[7], (DIM_Q, H * K), jnp.float32) / np.sqrt(H * K).astype(np.float32)}
    _L0_xattn_all = _L0_xattn_setup()
    _L0_xattn_in = {k: v for k, v in _L0_xattn_all.items() if k in ('Wq', 'w_kc_q', 'w_kc_kv', 'W_qr', 'W_kr', 'Wo')}
    del _L0_xattn_all

    def _L0_attn_setup():
        import jax, jax.numpy as jnp
        import numpy as np
        HEADS = 16
        key = jax.random.key(seed)
        ks = jax.random.split(key, 5)
        B, T, D = (2, 256, 256)
        s = 0.02
        return {'x': jax.random.normal(ks[0], (B, T, D), dtype=jnp.float32), 'Wq': jax.random.normal(ks[1], (D, D), dtype=jnp.float32) * s, 'Wk': jax.random.normal(ks[2], (D, D), dtype=jnp.float32) * s, 'Wv': jax.random.normal(ks[3], (D, D), dtype=jnp.float32) * s, 'Wo': jax.random.normal(ks[4], (D, D), dtype=jnp.float32) * s}
    _L0_attn_all = _L0_attn_setup()
    _L0_attn_in = {k: v for k, v in _L0_attn_all.items() if k in ('Wq', 'Wk', 'Wv', 'Wo')}
    del _L0_attn_all

    def _L0_ffn_setup():
        import jax, jax.numpy as jnp
        import numpy as np
        HIDDEN = 256
        INTER = 1024
        SCALE = 64.0

        def fwht(x):
            orig_shape = x.shape
            n = orig_shape[-1]
            x = x.reshape(-1, n)
            h = 1
            while h < n:
                x = x.reshape(-1, n // (2 * h), 2, h)
                a, b = (x[:, :, 0, :], x[:, :, 1, :])
                x = jnp.stack([a + b, a - b], axis=2).reshape(-1, n)
                h *= 2
            return (x / jnp.sqrt(jnp.asarray(n, x.dtype))).reshape(orig_shape)
        key = jax.random.key(seed)
        ks = jax.random.split(key, 8)
        inp = jax.random.normal(ks[0], (4, 256, HIDDEN), dtype=jnp.float32)
        SU_ug = jnp.where(jax.random.bernoulli(ks[1], 0.5, (HIDDEN,)), 1.0, -1.0).astype(jnp.float32)
        SU_dp = jnp.where(jax.random.bernoulli(ks[2], 0.5, (INTER,)), 1.0, -1.0).astype(jnp.float32)
        Wscale_ug = jax.random.uniform(ks[3], (2 * INTER,), jnp.float32, 0.5, 1.5)
        Wscale_dp = jax.random.uniform(ks[4], (HIDDEN,), jnp.float32, 0.5, 1.5)
        W_up = jax.random.normal(ks[5], (INTER, HIDDEN), dtype=jnp.float32) * 0.02
        W_gate = jax.random.normal(ks[6], (INTER, HIDDEN), dtype=jnp.float32) * 0.02
        W_down = jax.random.normal(ks[7], (HIDDEN, INTER), dtype=jnp.float32) * 0.02
        return {'input': inp, 'SU_ug': SU_ug, 'SU_dp': SU_dp, 'Wscale_ug': Wscale_ug, 'Wscale_dp': Wscale_dp, 'W_up': W_up, 'W_gate': W_gate, 'W_down': W_down}
    _L0_ffn_all = _L0_ffn_setup()
    _L0_ffn_in = {k: v for k, v in _L0_ffn_all.items() if k in ('SU_ug', 'SU_dp', 'Wscale_ug', 'Wscale_dp', 'W_up', 'W_gate', 'W_down')}
    del _L0_ffn_all

    def _L1_xattn_setup():
        import jax, jax.numpy as jnp
        import numpy as np
        B, S, H, NH, L = (2, 256, 256, 16, 64)
        HD = H // NH
        key = jax.random.key(seed)
        k1, k2, k3, k4, k5 = jax.random.split(key, 5)
        scale = 0.02
        return {'q': jax.random.normal(k1, (B, S, H), dtype=jnp.float32), 'latent_kv': jax.random.normal(k2, (B, S, L), dtype=jnp.float32), 'Wq': jax.random.normal(k3, (H, H), dtype=jnp.float32) * scale, 'Wkv_expand': jax.random.normal(k4, (2 * H, L), dtype=jnp.float32) * scale, 'Wout': jax.random.normal(k5, (H, H), dtype=jnp.float32) * scale}
    _L1_xattn_all = _L1_xattn_setup()
    _L1_xattn_in = {k: v for k, v in _L1_xattn_all.items() if k in ('Wq', 'Wkv_expand', 'Wout')}
    del _L1_xattn_all

    def _L1_attn_setup():
        import jax, jax.numpy as jnp
        import numpy as np
        B, S, HID = (2, 256, 256)
        HV, HK, DK, DV = (32, 16, 128, 128)
        KEY_DIM = HK * DK
        VAL_DIM = HV * DV
        CONV_DIM = 2 * KEY_DIM + VAL_DIM
        KS = 4
        EPS = 1e-06

        def _l2norm(x):
            return x / jnp.maximum(jnp.linalg.norm(x, axis=-1, keepdims=True), EPS)
        key = jax.random.key(seed)
        ks = jax.random.split(key, 8)
        s = lambda k, shape, scale: jax.random.normal(k, shape, dtype=jnp.float32) * scale
        return {'hidden_states': s(ks[0], (B, S, HID), 1.0), 'W_qkv': s(ks[1], (CONV_DIM, HID), 0.02), 'W_z': s(ks[2], (VAL_DIM, HID), 0.02), 'W_a': s(ks[3], (HV, HID), 0.02), 'W_b': s(ks[4], (HV, HID), 0.02), 'conv_w': s(ks[5], (CONV_DIM, KS), 0.2), 'A_log': jnp.zeros((HV,), jnp.float32), 'dt_bias': jnp.ones((HV,), jnp.float32), 'norm_w': jnp.ones((DV,), jnp.float32), 'W_out': s(ks[6], (HID, VAL_DIM), 0.02)}
    _L1_attn_all = _L1_attn_setup()
    _L1_attn_in = {k: v for k, v in _L1_attn_all.items() if k in ('W_qkv', 'W_z', 'W_a', 'W_b', 'conv_w', 'A_log', 'dt_bias', 'norm_w', 'W_out')}
    del _L1_attn_all

    def _L1_ffn_setup():
        import jax, jax.numpy as jnp
        import numpy as np
        E, TOP_K, H, I = (32, 8, 256, 96)
        B, S = (1, 256)
        key = jax.random.key(seed)
        ks = jax.random.split(key, 5)
        scale = 0.02
        return {'hidden_states': jax.random.normal(ks[0], (B, S, H), dtype=jnp.float32), 'gate_w': jax.random.normal(ks[1], (E, H), dtype=jnp.float32) * scale, 'Wg': jax.random.normal(ks[2], (E, I, H), dtype=jnp.float32) * scale, 'Wu': jax.random.normal(ks[3], (E, I, H), dtype=jnp.float32) * scale, 'Wd': jax.random.normal(ks[4], (E, H, I), dtype=jnp.float32) * scale}
    _L1_ffn_all = _L1_ffn_setup()
    _L1_ffn_in = {k: v for k, v in _L1_ffn_all.items() if k in ('gate_w', 'Wg', 'Wu', 'Wd')}
    del _L1_ffn_all
    return {'x': x, 'ctx_512': ctx_512, 'L0_xattn_Wq': _L0_xattn_in['Wq'], 'L0_xattn_w_kc_q': _L0_xattn_in['w_kc_q'], 'L0_xattn_w_kc_kv': _L0_xattn_in['w_kc_kv'], 'L0_xattn_W_qr': _L0_xattn_in['W_qr'], 'L0_xattn_W_kr': _L0_xattn_in['W_kr'], 'L0_xattn_Wo': _L0_xattn_in['Wo'], 'L0_attn_Wq': _L0_attn_in['Wq'], 'L0_attn_Wk': _L0_attn_in['Wk'], 'L0_attn_Wv': _L0_attn_in['Wv'], 'L0_attn_Wo': _L0_attn_in['Wo'], 'L0_ffn_SU_ug': _L0_ffn_in['SU_ug'], 'L0_ffn_SU_dp': _L0_ffn_in['SU_dp'], 'L0_ffn_Wscale_ug': _L0_ffn_in['Wscale_ug'], 'L0_ffn_Wscale_dp': _L0_ffn_in['Wscale_dp'], 'L0_ffn_W_up': _L0_ffn_in['W_up'], 'L0_ffn_W_gate': _L0_ffn_in['W_gate'], 'L0_ffn_W_down': _L0_ffn_in['W_down'], 'L1_xattn_Wq': _L1_xattn_in['Wq'], 'L1_xattn_Wkv_expand': _L1_xattn_in['Wkv_expand'], 'L1_xattn_Wout': _L1_xattn_in['Wout'], 'L1_attn_W_qkv': _L1_attn_in['W_qkv'], 'L1_attn_W_z': _L1_attn_in['W_z'], 'L1_attn_W_a': _L1_attn_in['W_a'], 'L1_attn_W_b': _L1_attn_in['W_b'], 'L1_attn_conv_w': _L1_attn_in['conv_w'], 'L1_attn_A_log': _L1_attn_in['A_log'], 'L1_attn_dt_bias': _L1_attn_in['dt_bias'], 'L1_attn_norm_w': _L1_attn_in['norm_w'], 'L1_attn_W_out': _L1_attn_in['W_out'], 'L1_ffn_gate_w': _L1_ffn_in['gate_w'], 'L1_ffn_Wg': _L1_ffn_in['Wg'], 'L1_ffn_Wu': _L1_ffn_in['Wu'], 'L1_ffn_Wd': _L1_ffn_in['Wd']}

def reference(x, ctx_512, L0_xattn_Wq, L0_xattn_w_kc_q, L0_xattn_w_kc_kv, L0_xattn_W_qr, L0_xattn_W_kr, L0_xattn_Wo, L0_attn_Wq, L0_attn_Wk, L0_attn_Wv, L0_attn_Wo, L0_ffn_SU_ug, L0_ffn_SU_dp, L0_ffn_Wscale_ug, L0_ffn_Wscale_dp, L0_ffn_W_up, L0_ffn_W_gate, L0_ffn_W_down, L1_xattn_Wq, L1_xattn_Wkv_expand, L1_xattn_Wout, L1_attn_W_qkv, L1_attn_W_z, L1_attn_W_a, L1_attn_W_b, L1_attn_conv_w, L1_attn_A_log, L1_attn_dt_bias, L1_attn_norm_w, L1_attn_W_out, L1_ffn_gate_w, L1_ffn_Wg, L1_ffn_Wu, L1_ffn_Wd):
    import jax
    import jax.numpy as jnp

    def _L0_xattn_ref(hidden_q, kv_c, Wq, w_kc_q, w_kc_kv, W_qr, W_kr, Wo):
        import jax, jax.numpy as jnp
        import numpy as np
        B, S, L = (2, 128, 128)
        DIM_Q, H, K, D_C, D_CQ, R = (256, 16, 128, 64, 192, 64)

        def _rope_tables(length, dim):
            inv = 1.0 / 10000.0 ** (jnp.arange(0, dim, 2, dtype=jnp.float32) / dim)
            f = jnp.arange(length, dtype=jnp.float32)[:, None] * inv[None, :]
            sin = jnp.repeat(jnp.sin(f), 2, axis=-1)
            cos = jnp.repeat(jnp.cos(f), 2, axis=-1)
            return (sin, cos)

        def _rotate_half(x):
            half = x.shape[-1] // 2
            return jnp.concatenate([-x[..., half:], x[..., :half]], axis=-1)

        def _apply_rope(x, sin, cos):
            return x * cos + _rotate_half(x) * sin
        Bv, Sv, _ = hidden_q.shape
        _, Lv, _ = kv_c.shape
        q_hk = (hidden_q @ Wq.T).reshape(Bv, Sv, H, K)
        q_big = jnp.einsum('bshk,hkq->bshq', q_hk, w_kc_q)
        sin_q, cos_q = _rope_tables(Sv, D_CQ)
        q_big = _apply_rope(q_big, sin_q[None, :, None, :], cos_q[None, :, None, :])
        sin_k, cos_k = _rope_tables(Lv, D_C)
        kv_r = _apply_rope(kv_c, sin_k[None], cos_k[None])
        q_r = jnp.einsum('bshq,hqr->bhsr', q_big, W_qr)
        k_r = jnp.einsum('bld,hdr->bhlr', kv_r, W_kr)
        scores = jnp.einsum('bhsr,bhlr->bhsl', q_r, k_r)
        attn = jax.nn.softmax(scores, axis=-1)
        ctx_c = jnp.einsum('bhsl,bld->bhsd', attn, kv_r)
        ctx_lat = jnp.einsum('bhsd,hkd->bhsk', ctx_c, w_kc_kv)
        ctx = ctx_lat.transpose(0, 2, 1, 3).reshape(Bv, Sv, H * K)
        return ctx @ Wo.T

    def _L0_attn_ref(x, Wq, Wk, Wv, Wo):
        import jax, jax.numpy as jnp
        import numpy as np
        HEADS = 16
        B, T, _ = x.shape
        H = HEADS
        Dh = Wq.shape[1] // H
        q = (x @ Wq).reshape(B, T, H, Dh)
        k = (x @ Wk).reshape(B, T, H, Dh)
        v = (x @ Wv).reshape(B, T, H, Dh)
        scores = jnp.einsum('bthd,bshd->bhts', q, k)
        mask = jnp.tril(jnp.ones((T, T), dtype=scores.dtype))
        scores = scores * mask
        attn = jax.nn.softmax(scores / T ** 0.5, axis=-1)
        out = jnp.einsum('bhts,bshd->bthd', attn, v).reshape(B, T, H * Dh)
        return out @ Wo

    def _L0_ffn_ref(input, SU_ug, SU_dp, Wscale_ug, Wscale_dp, W_up, W_gate, W_down):
        import jax, jax.numpy as jnp
        import numpy as np
        HIDDEN = 256
        INTER = 1024
        SCALE = 64.0

        def fwht(x):
            orig_shape = x.shape
            n = orig_shape[-1]
            x = x.reshape(-1, n)
            h = 1
            while h < n:
                x = x.reshape(-1, n // (2 * h), 2, h)
                a, b = (x[:, :, 0, :], x[:, :, 1, :])
                x = jnp.stack([a + b, a - b], axis=2).reshape(-1, n)
                h *= 2
            return (x / jnp.sqrt(jnp.asarray(n, x.dtype))).reshape(orig_shape)
        n = SU_ug.shape[0]
        x = input.reshape(-1, n)
        x = fwht(x * SU_ug) / SCALE
        x_up = x @ W_up.T * (Wscale_ug[:INTER] * SCALE)
        x_gate = x @ W_gate.T * (Wscale_ug[INTER:] * SCALE)
        x = jax.nn.silu(x_gate) * x_up
        x = fwht(x * SU_dp) / SCALE
        x = x @ W_down.T * (Wscale_dp * SCALE)
        return x.reshape(input.shape)

    def _L1_xattn_ref(q, latent_kv, Wq, Wkv_expand, Wout):
        import jax, jax.numpy as jnp
        import numpy as np
        B, S, H, NH, L = (2, 256, 256, 16, 64)
        HD = H // NH
        b, sq, _ = q.shape
        sk = latent_kv.shape[1]
        qp = q @ Wq.T
        kv = latent_kv @ Wkv_expand.T
        k, v = jnp.split(kv, 2, axis=-1)
        qh = qp.reshape(b, sq, NH, HD).transpose(0, 2, 1, 3)
        kh = k.reshape(b, sk, NH, HD).transpose(0, 2, 1, 3)
        vh = v.reshape(b, sk, NH, HD).transpose(0, 2, 1, 3)
        inv_sqrt_d = 1.0 / jnp.sqrt(jnp.float32(HD))
        scores = jnp.einsum('bhqd,bhkd->bhqk', qh, kh) * inv_sqrt_d
        causal = jnp.tril(jnp.ones((sq, sk), dtype=bool))
        scores = jnp.where(causal, scores, jnp.finfo(scores.dtype).min)
        attn = jax.nn.softmax(scores, axis=-1)
        out = jnp.einsum('bhqk,bhkd->bhqd', attn, vh)
        out = out.transpose(0, 2, 1, 3).reshape(b, sq, H)
        return out @ Wout.T

    def _L1_attn_ref(hidden_states, W_qkv, W_z, W_a, W_b, conv_w, A_log, dt_bias, norm_w, W_out):
        import jax, jax.numpy as jnp
        import numpy as np
        B, S, HID = (2, 256, 256)
        HV, HK, DK, DV = (32, 16, 128, 128)
        KEY_DIM = HK * DK
        VAL_DIM = HV * DV
        CONV_DIM = 2 * KEY_DIM + VAL_DIM
        KS = 4
        EPS = 1e-06

        def _l2norm(x):
            return x / jnp.maximum(jnp.linalg.norm(x, axis=-1, keepdims=True), EPS)
        Bn, Sn, _ = hidden_states.shape
        qkv = hidden_states @ W_qkv.T
        z = hidden_states @ W_z.T
        a = hidden_states @ W_a.T
        b = hidden_states @ W_b.T
        xp = jnp.pad(qkv, ((0, 0), (KS - 1, 0), (0, 0)))
        conv = sum((xp[:, k:k + Sn, :] * conv_w[:, k] for k in range(KS)))
        mixed = jax.nn.silu(conv)
        q = mixed[..., :KEY_DIM].reshape(Bn, Sn, HK, DK)
        k = mixed[..., KEY_DIM:2 * KEY_DIM].reshape(Bn, Sn, HK, DK)
        v = mixed[..., 2 * KEY_DIM:].reshape(Bn, Sn, HV, DV)
        rep = HV // HK
        q = jnp.repeat(q, rep, axis=2)
        k = jnp.repeat(k, rep, axis=2)
        q = _l2norm(q) * DK ** (-0.5)
        k = _l2norm(k)
        g = -jnp.exp(A_log) * jax.nn.softplus(a + dt_bias)
        beta = jax.nn.sigmoid(b)
        qs = q.transpose(1, 0, 2, 3)
        ks_ = k.transpose(1, 0, 2, 3)
        vs = v.transpose(1, 0, 2, 3)
        gs = g.transpose(1, 0, 2)
        bs = beta.transpose(1, 0, 2)

        def step(state, inp):
            qt, kt, vt, gt, bt = inp
            state = state * jnp.exp(gt)[..., None, None]
            kv = jnp.einsum('bhk,bhkv->bhv', kt, state)
            delta = (vt - kv) * bt[..., None]
            state = state + jnp.einsum('bhk,bhv->bhkv', kt, delta)
            out = jnp.einsum('bhk,bhkv->bhv', qt, state)
            return (state, out)
        state0 = jnp.zeros((Bn, HV, DK, DV), hidden_states.dtype)
        _, outs = jax.lax.scan(step, state0, (qs, ks_, vs, gs, bs))
        o = outs.transpose(1, 0, 2, 3)
        var = jnp.mean(jnp.square(o), axis=-1, keepdims=True)
        o = o * jax.lax.rsqrt(var + EPS) * norm_w
        o = o * jax.nn.silu(z.reshape(Bn, Sn, HV, DV))
        return o.reshape(Bn, Sn, VAL_DIM) @ W_out.T

    def _L1_ffn_ref(hidden_states, gate_w, Wg, Wu, Wd):
        import jax, jax.numpy as jnp
        import numpy as np
        E, TOP_K, H, I = (32, 8, 256, 96)
        B, S = (1, 256)
        b, s, h = hidden_states.shape
        x = hidden_states.reshape(-1, h)
        T = x.shape[0]
        router_logits = x @ gate_w.T
        probs = jax.nn.softmax(router_logits.astype(jnp.float32), axis=-1)
        top_vals, top_idx = jax.lax.top_k(probs, TOP_K)
        top_vals = top_vals / jnp.sum(top_vals, axis=-1, keepdims=True)
        top_vals = top_vals.astype(hidden_states.dtype)
        routing_matrix = jnp.zeros_like(router_logits).at[jnp.arange(T)[:, None], top_idx].set(top_vals)
        g = jnp.einsum('th,eih->eti', x, Wg)
        u = jnp.einsum('th,eih->eti', x, Wu)
        expert_out = jnp.einsum('eti,ehi->eth', jax.nn.silu(g) * u, Wd)
        out = jnp.einsum('te,eth->th', routing_matrix, expert_out)
        return out.reshape(b, s, h)
    x = x + _L0_xattn_ref(_layernorm(x, axis=-1), ctx_512, L0_xattn_Wq, L0_xattn_w_kc_q, L0_xattn_w_kc_kv, L0_xattn_W_qr, L0_xattn_W_kr, L0_xattn_Wo)
    x = x + _L0_attn_ref(_layernorm(x, axis=-1), L0_attn_Wq, L0_attn_Wk, L0_attn_Wv, L0_attn_Wo)
    x = x + _L0_ffn_ref(_layernorm(x, axis=-1), L0_ffn_SU_ug, L0_ffn_SU_dp, L0_ffn_Wscale_ug, L0_ffn_Wscale_dp, L0_ffn_W_up, L0_ffn_W_gate, L0_ffn_W_down)
    x = x + _L1_xattn_ref(_layernorm(x, axis=-1), ctx_512, L1_xattn_Wq, L1_xattn_Wkv_expand, L1_xattn_Wout)
    x = x + _L1_attn_ref(_layernorm(x, axis=-1), L1_attn_W_qkv, L1_attn_W_z, L1_attn_W_a, L1_attn_W_b, L1_attn_conv_w, L1_attn_A_log, L1_attn_dt_bias, L1_attn_norm_w, L1_attn_W_out)
    x = x + _L1_ffn_ref(_layernorm(x, axis=-1), L1_ffn_gate_w, L1_ffn_Wg, L1_ffn_Wu, L1_ffn_Wd)
    return x

_drawn_inputs = setup_inputs


def setup_inputs(seed=0):
    import zlib

    import numpy as np

    out = dict(_drawn_inputs(seed))
    spreads = {'L1_attn_A_log': (0.0, 2.0), 'L1_attn_dt_bias': (1.0, 0.6), 'L1_attn_norm_w': (1.0, 0.6)}
    factors = {'L0_attn_Wq': 8.0,
     'L0_attn_Wk': 8.0,
     'L0_ffn_Wscale_ug': 4.14,
     'L0_ffn_Wscale_dp': 5.759,
     'L1_xattn_Wq': 64.0,
     'L1_attn_W_a': 103.334,
     'L1_attn_W_b': 22.379,
     'L1_ffn_gate_w': 8.0,
     'L1_ffn_Wg': 8.0,
     'L1_ffn_Wu': 8.0,
     'L1_ffn_Wd': 8.0,
     'L1_xattn_Wkv_expand': 4.982,
     'L1_xattn_Wout': 4.71}
    for name, (base, spread) in spreads.items():
        noise = np.random.default_rng([zlib.crc32(name.encode()), seed]).standard_normal(out[name].shape)
        drawn = base * np.exp(spread * noise) if base else spread * noise
        out[name] = jnp.asarray(drawn.astype(out[name].dtype))
    for name, factor in factors.items():
        out[name] = (out[name] * factor).astype(out[name].dtype)
    return out
```

```python
import numpy as np
import concourse.bass as bass
from concourse import mybir
from contextlib import ExitStack

F32 = mybir.dt.float32
ALU = mybir.AluOpType
ACT = mybir.ActivationFunctionType
AX = mybir.AxisListType

P = 128
B, S, D = 16, 64, 256
TILES = B * S // P
DC = D // P
L, DCTX = 128, 64
H0, K0, CQ, R0 = 16, 128, 192, 64
HQ = CQ // 2
NH, HD = 16, 16
PAIRS = NH // 2
INTER = 1024
IC = INTER // P
HK, HV, DK = 16, 32, 128
NE, TOPK, EI = 32, 8, 96
MC = NE * EI // P
MB = NE * EI // 512
LEVELS = 6
BIG = 1e30


def shape_constants():
    cols, at = [], {}

    def put(name, a):
        a = np.asarray(a, np.float32)
        full = np.zeros((P, a.shape[1]), np.float32)
        full[:a.shape[0]] = a
        at[name] = (sum(c.shape[1] for c in cols), a.shape[1])
        cols.append(full)

    def rope(length, dim):
        inv = (np.float32(1.0) / np.float32(10000.0) ** (np.arange(0, dim, 2, dtype=np.float32) / np.float32(dim))).astype(np.float32)
        f = np.arange(length, dtype=np.float32)[:, None] * inv[None, :]
        return np.repeat(np.sin(f), 2, axis=-1), np.repeat(np.cos(f), 2, axis=-1)

    i, j = np.arange(P)[:, None], np.arange(P)[None, :]
    t, s = np.arange(P)[:, None] % S, np.arange(S)[None, :]
    put("ident", i == j)
    put("cumsum", (i <= j) & (i // S == j // S))
    had = np.array([[(-1.0) ** bin(a & b).count("1") for b in range(P)] for a in range(P)])
    put("had", had)
    put("nhad", -had)
    put("eye", t == s)
    put("tril", t >= s)
    put("strict", t > s)
    put("neg", np.where(t >= s, 0.0, -BIG))
    for k in range(LEVELS):
        w = 1 << k
        put(f"lvl{k}", (t // (2 * w) == s // (2 * w)) & (t // w % 2 == 1) & (s // w % 2 == 0))
    put("head", np.arange(P)[:, None] // HD == np.arange(P // HD)[None, :])
    put("mhalf", np.full((P, 32), -0.5))
    put("ones", np.ones((P, 1)))
    sq, cq = rope(S, CQ)
    put("cosq", np.concatenate([cq[:, :HQ].T, cq[:, HQ:].T], axis=1))
    put("sinq", np.concatenate([sq[:, :HQ].T, sq[:, HQ:].T], axis=1))
    sk, ck = rope(L, DCTX)
    sk = sk * np.where(np.arange(DCTX) < DCTX // 2, -1.0, 1.0)
    put("cosk", ck)
    put("sink", sk)
    put("coskT", ck.T)
    put("sinkT", sk.T)
    return np.concatenate(cols, axis=1), at


CONSTS, CONST_AT = shape_constants()


def build(nc, d, out, phases=5):
    root = ExitStack()
    with root:
        def sb(ctx, name, shape):
            return ctx.enter_context(nc.sbuf_tensor(name, shape, F32))

        def semaphores(ctx, names, phase=""):
            made = {n: nc.alloc_semaphore(phase + n) for n in names.split()}

            def retire():
                nc.clear_and_free_semaphores(list(made.values()))
                nc.all_engine_barrier()

            ctx.callback(retire)
            return made

        X = sb(root, "X", [P, TILES, D])
        con = sb(root, "con", [P, CONSTS.shape[1]])
        HT = sb(root, "HT", [P, DC, B * S])
        bn = sb(root, "bn", [P, 2, 6])
        mv = sb(root, "mv", [P, 2, 2])
        ve = sb(root, "ve", [P, 2, 1])
        rstd = sb(root, "rstd", [P, 2, 1])
        hn = sb(root, "hn", [P, 2, D])
        carrier = sb(root, "carrier", [P, 1])
        PS = root.enter_context(nc.psum_tensor("PS", [P, 8, 512], F32))

        def C(name, rows=P):
            o, n = CONST_AT[name]
            return con[0:rows, o:o + n]

        def over(ap, n):
            return ap.unsqueeze(1).broadcast_to([ap.shape[0], n, ap.shape[1]])

        def each(ap, n):
            return ap.unsqueeze(2).broadcast_to([ap.shape[0], ap.shape[1], n])

        def norm_stats(v, i, p, stats, n):
            v.bn_stats(bn[:, p, :], X[:, bass.ds(i * 2 + p, 1), :]).then_inc(stats, 1)
            v.wait_ge(stats, n * 4 + 1)
            v.memset(carrier[:, :], 0.0)
            v.bn_aggr(mv[:, p, :], bn[:, p, :]).then_inc(stats, 1)
            v.wait_ge(stats, n * 4 + 2)
            v.tensor_scalar(ve[:, p, :], mv[:, p, 1:2], 1e-5, None, ALU.add).then_inc(stats, 1)

        def norm_root(g, n, p, stats, rooted):
            g.wait_ge(stats, n * 4 + 3)
            g.tensor_tensor(rstd[:, p, :], ve[:, p, :], C("mhalf")[:, 0:1], ALU.pow).then_inc(rooted, 1)

        def norm_apply(v, i, p, stats, rooted, turned, n):
            v.wait_ge(turned, n + 1)
            v.wait_ge(rooted, n + 1)
            v.tensor_scalar(hn[:, p, :], X[:, bass.ds(i * 2 + p, 1), :], mv[:, p, 0:1], rstd[:, p, :],
                            ALU.subtract, ALU.mult).then_inc(stats, 1)

        def norm_turn(pe, n, p, bank, stats, turned):
            pe.wait_ge(stats, n * 4 + 4)
            for c in range(DC):
                mm = pe.transpose(PS[:, bank, c * P:(c + 1) * P], hn[:, p, c * P:(c + 1) * P], C("ident"))
            mm.then_inc(turned, 1)

        def hT_psum(bank):
            return PS[:, bank, 0:D].rearrange("p (c n) -> p c n", c=DC)

        mid = root.enter_context(ExitStack())
        kvr = sb(mid, "kvr", [P, B, DCTX])
        kvT = sb(mid, "kvT", [DCTX, B, L])
        cxT = sb(mid, "cxT", [DCTX, B, L])
        TTd = nc.dram_tensor("queries_scratch", (DCTX, B, H0, S), F32, kind="Internal").ap()
        W2 = sb(mid, "W2", [P, H0 // 2, D])
        with ExitStack() as ctx:
            cxr = sb(ctx, "cxr", [DCTX, B, L])
            cx = sb(ctx, "cx", [P, B, DCTX])
            cr = sb(ctx, "cr", [P, B, DCTX])
            s = semaphores(ctx, "p0_in p0_x p0_kv p0_dve p0_stats0 p0_stats1 p0_root0 p0_root1 p0_turned0 p0_turned1 p0_hT0 p0_hT1")
            with nc.Block() as block:
                @block.sync
                def _(sp):
                    sp.dma_start(con[:, :], d["consts"]).then_inc(s["p0_x"], 16)
                    sp.dma_start(X[:, :, :], d["x"].rearrange("(n b) s c -> (b s) n c", b=2)).then_inc(s["p0_x"], 16)
                    sp.dma_start(cxT[:, :, :], d["ctxT"]).then_inc(s["p0_in"], 16)
                    sp.dma_start(cxr[:, :, :], d["ctxT_rolled"]).then_inc(s["p0_in"], 16)
                    sp.dma_start(cx[:, :, :], d["ctx"]).then_inc(s["p0_in"], 16)
                    sp.dma_start(cr[:, :, :], d["ctx_rolled"]).then_inc(s["p0_in"], 16)

                @block.vector
                def _(v):
                    v.wait_ge(s["p0_x"], 32)
                    with v.Fori(0, TILES // 2) as i:
                        for p in range(2):
                            norm_stats(v, i, p, s[f"p0_stats{p}"], i)
                        for p in range(2):
                            norm_apply(v, i, p, s[f"p0_stats{p}"], s[f"p0_root{p}"], s[f"p0_turned{p}"], i)
                    v.wait_ge(s["p0_in"], 64)
                    v.tensor_tensor(kvT[:, :, :], cxT[:, :, :], over(C("coskT", DCTX), B), ALU.mult).then_inc(s["p0_dve"], 1)
                    v.tensor_tensor(cxr[:, :, :], cxr[:, :, :], over(C("sinkT", DCTX), B), ALU.mult).then_inc(s["p0_dve"], 1)
                    v.tensor_tensor(kvr[:, :, :], cx[:, :, :], over(C("cosk"), B), ALU.mult).then_inc(s["p0_dve"], 1)
                    v.tensor_tensor(cr[:, :, :], cr[:, :, :], over(C("sink"), B), ALU.mult).then_inc(s["p0_dve"], 1)
                    v.wait_ge(s["p0_dve"], 2)
                    v.tensor_tensor(kvT[:, :, :], kvT[:, :, :], cxr[:, :, :], ALU.add).then_inc(s["p0_kv"], 1)
                    v.wait_ge(s["p0_dve"], 4)
                    v.tensor_tensor(kvr[:, :, :], kvr[:, :, :], cr[:, :, :], ALU.add).then_inc(s["p0_kv"], 1)

                @block.gpsimd
                def _(g):
                    g.wait_ge(s["p0_x"], 32)
                    with g.Fori(0, TILES // 2) as i:
                        for p in range(2):
                            norm_root(g, i, p, s[f"p0_stats{p}"], s[f"p0_root{p}"])

                @block.tensor
                def _(pe):
                    for p in range(2):
                        pe.sem_inc(s[f"p0_turned{p}"], 1)
                    with pe.Fori(0, TILES // 2) as i:
                        for p in range(2):
                            pe.wait_ge(s[f"p0_hT{p}"], i + 1)
                            norm_turn(pe, i, p, p, s[f"p0_stats{p}"], s[f"p0_turned{p}"])

                @block.scalar
                def _(a):
                    for p in range(2):
                        a.sem_inc(s[f"p0_hT{p}"], 1)
                    with a.Fori(0, TILES // 2) as i:
                        for p in range(2):
                            a.wait_ge(s[f"p0_turned{p}"], i + 2)
                            a.activation(HT[:, :, bass.ds(i * 2 * P + p * P, P)], hT_psum(p), ACT.Copy).then_inc(s[f"p0_hT{p}"], 1)

        KW = D + CQ + DCTX + D
        RW = CQ + DCTX
        if phases >= 1:
          with ExitStack() as ctx:
            wk = sb(ctx, "wk", [P, 2, KW])
            tts = sb(ctx, "tts", [DCTX, 2, 512])
            wr = sb(ctx, "wr", [R0, 2, RW])
            cw = sb(ctx, "cw", [P, 2, DC, CQ])
            mw = sb(ctx, "mw", [HQ, 2, 2, DCTX])
            ra = sb(ctx, "ra", [HQ, 2, 512])
            rb = sb(ctx, "rb", [HQ, 2, 512])
            rc = sb(ctx, "rc", [HQ, 2, 512])
            rd = sb(ctx, "rd", [HQ, 2, 512])
            r0 = sb(ctx, "r0", [HQ, 2, 512])
            r1 = sb(ctx, "r1", [HQ, 2, 512])
            s = semaphores(ctx, "p1_w0 p1_w1 p1_c p1_mw p1_w2 p1_cs p1_ms p1_w2s p1_q0 p1_q1 p1_prod0 p1_prod1 p1_rope0 p1_rope1 p1_t0 p1_t1 p1_ts0 p1_ts1 p1_st0 p1_st1")
            with nc.Block() as block:
                @block.sync
                def _(sp):
                    def load(h, p):
                        sp.dma_start(wk[:, p, :], d["l0x_k"][bass.ds(h, 1), :, :].rearrange("a p n -> (a p) n")).then_inc(s[f"p1_w{p}"], 16)
                        sp.dma_start(wr[:, p, :], d["l0x_r"][bass.ds(h, 1), :, :].rearrange("a p n -> (a p) n")).then_inc(s[f"p1_w{p}"], 16)
                    for p in range(2):
                        load(p, p)
                        sp.sem_inc(s[f"p1_st{p}"], 16)

                    def store(h):
                        for f in range(2):
                            sp.wait_ge(s[f"p1_ts{f}"], h + 2)
                            sp.dma_start(TTd[:, f * 8:(f + 1) * 8, bass.ds(h, 1), :].rearrange("p b a s -> p b (a s)"), tts[:, f, :].rearrange("p (b s) -> p b s", s=S)).then_inc(s[f"p1_st{f}"], 16)

                    with sp.Fori(0, H0 // 2 - 1) as i:
                        for p in range(2):
                            sp.wait_ge(s["p1_w2"], i * 2 + p + 1)
                            load(i * 2 + p + 2, p)
                            store(i * 2 + p)
                    for h in (H0 - 2, H0 - 1):
                        store(h)
                    for f in range(2):
                        sp.wait_ge(s[f"p1_st{f}"], H0 * 16 + 16)

                @block.tensor
                def _(pe):
                    for f in range(2):
                        pe.sem_inc(s[f"p1_t{f}"], 1)
                    with pe.Fori(0, H0 // 2) as i:
                        for p in range(2):
                            h = i * 2 + p
                            pe.wait_ge(s[f"p1_w{p}"], i * 32 + 32)
                            pe.wait_ge(s["p1_w2s"], h + 1)
                            for c in range(DC):
                                mm = pe.matmul(PS[:, 0, c * CQ:(c + 1) * CQ], wk[:, p, c * P:(c + 1) * P],
                                               wk[:, p, D:D + CQ], start=True, stop=True)
                            mm.then_inc(s["p1_c"], 1)
                            for c in range(2):
                                mm = pe.matmul(PS[0:HQ, 1, c * DCTX:(c + 1) * DCTX], wr[:, p, c * HQ:(c + 1) * HQ],
                                               wr[:, p, CQ:RW], start=True, stop=True)
                            mm.then_inc(s["p1_mw"], 1)
                            pe.matmul(PS[64 * p:64 * p + DCTX, 1, P:P + D], wk[:, p, D + CQ:D + CQ + DCTX],
                                      wk[:, p, D + CQ + DCTX:KW], start=True, stop=True).then_inc(s["p1_w2"], 1)
                            pe.wait_ge(s["p1_cs"], h + 1)
                            for f in range(2):
                                for c in range(2):
                                    for k in range(DC):
                                        mm = pe.matmul(PS[0:HQ, 2 + 2 * f + c, :], cw[:, p, k, c * HQ:(c + 1) * HQ],
                                                       HT[:, k, f * 512:(f + 1) * 512], start=(k == 0), stop=(k == DC - 1))
                                mm.then_inc(s[f"p1_q{f}"], 1)
                            pe.wait_ge(s["p1_ms"], h + 1)
                            for f in range(2):
                                pe.wait_ge(s[f"p1_rope{f}"], h * 2 + 2)
                                pe.wait_ge(s[f"p1_ts{f}"], h + 1)
                                pe.matmul(PS[0:DCTX, 6 + f, :], mw[:, p, 0, :], r0[:, f, :], start=True, stop=False)
                                pe.matmul(PS[0:DCTX, 6 + f, :], mw[:, p, 1, :], r1[:, f, :], start=False, stop=True).then_inc(s[f"p1_t{f}"], 1)

                @block.scalar
                def _(a):
                    a.sem_inc(s["p1_w2s"], 1)
                    for f in range(2):
                        a.sem_inc(s[f"p1_ts{f}"], 1)
                    with a.Fori(0, H0 // 2) as i:
                        for p in range(2):
                            h = i * 2 + p
                            a.wait_ge(s["p1_c"], h + 1)
                            a.activation(cw[:, p, :, :], PS[:, 0, 0:DC * CQ].rearrange("p (c n) -> p c n", c=DC), ACT.Copy).then_inc(s["p1_cs"], 1)
                            a.wait_ge(s["p1_w2"], h + 1)
                            a.activation(mw[:, p, :, :], PS[0:HQ, 1, 0:2 * DCTX].rearrange("p (c n) -> p c n", c=2), ACT.Copy).then_inc(s["p1_ms"], 1)
                            a.activation(W2[64 * p:64 * p + DCTX, bass.ds(i, 1), :], PS[64 * p:64 * p + DCTX, 1, P:P + D].unsqueeze(1), ACT.Copy).then_inc(s["p1_w2s"], 1)
                            for f in range(2):
                                a.wait_ge(s[f"p1_t{f}"], h + 2)
                                a.wait_ge(s[f"p1_st{f}"], h * 16 + 16)
                                a.activation(tts[:, f, :], PS[0:DCTX, 6 + f, :], ACT.Copy).then_inc(s[f"p1_ts{f}"], 1)

                @block.vector
                def _(v):
                    def table(name, c):
                        return over(C(name, HQ)[:, c * S:(c + 1) * S], 512 // S)

                    def view(ap):
                        return ap.rearrange("p (b s) -> p b s", s=S)

                    with v.Fori(0, H0 // 2) as i:
                        for p in range(2):
                            h = i * 2 + p
                            for f in range(2):
                                prod, rope = s[f"p1_prod{f}"], s[f"p1_rope{f}"]
                                q0, q1 = view(PS[0:HQ, 2 + 2 * f, :]), view(PS[0:HQ, 3 + 2 * f, :])
                                v.wait_ge(s[f"p1_q{f}"], h + 1)
                                v.wait_ge(s[f"p1_t{f}"], h + 1)
                                v.tensor_tensor(view(ra[:, f, :]), q0, table("cosq", 0), ALU.mult).then_inc(prod, 1)
                                v.tensor_tensor(view(rb[:, f, :]), q1, table("sinq", 0), ALU.mult).then_inc(prod, 1)
                                v.tensor_tensor(view(rc[:, f, :]), q1, table("cosq", 1), ALU.mult).then_inc(prod, 1)
                                v.tensor_tensor(view(rd[:, f, :]), q0, table("sinq", 1), ALU.mult).then_inc(prod, 1)
                                v.wait_ge(prod, h * 4 + 2)
                                v.tensor_tensor(r0[:, f, :], ra[:, f, :], rb[:, f, :], ALU.subtract).then_inc(rope, 1)
                                v.wait_ge(prod, h * 4 + 4)
                                v.tensor_tensor(r1[:, f, :], rc[:, f, :], rd[:, f, :], ALU.add).then_inc(rope, 1)

        if phases >= 2:
            phase2(nc, d, sb, semaphores, C, over, each, X, HT, PS, carrier, bn, mv, ve, rstd, hn, kvr, kvT, cxT, TTd, W2,
                   norm_stats, norm_root, norm_apply, norm_turn, hT_psum)
        mid.close()
        if phases >= 3 and phases != 9:
            phase3(nc, d, sb, semaphores, C, over, each, X, HT, PS, carrier)
        if phases >= 4:
            phase4(nc, d, sb, semaphores, C, over, each, X, PS, carrier, norm_stats, norm_root, norm_apply, norm_turn, hT_psum)

        with ExitStack() as ctx:
            s = semaphores(ctx, "stored")
            with nc.Block() as block:
                @block.sync
                def _(sp):
                    sp.dma_start(out.rearrange("(n b) s c -> (b s) n c", b=2), X[:, :, :]).then_inc(s["stored"], 16)
                    sp.wait_ge(s["stored"], 16)


def phase2(nc, d, sb, semaphores, C, over, each, X, HT, PS, carrier, bn, mv, ve, rstd, hn, kvr, kvT, cxT, TTd, W2,
           norm_stats, norm_root, norm_apply, norm_turn, hT_psum):
    PER_P = ("tt sc sm ex nr tp pt cx ct out res "
             "qkv q vv kb asc asm aex anr atp apt av ot aout ares "
             "stats root turned hT "
             "fx fh fhs ug th fy fo fres")
    with ExitStack() as ctx:
        aw = sb(ctx, "aw", [P, DC, 4 * D])
        xw = sb(ctx, "xw", [P, DC, 2 * D])
        xkv = sb(ctx, "xkv", [DCTX, 2 * D])
        ug = sb(ctx, "ug", [P, DC, 2 * INTER])
        dn = sb(ctx, "dn", [P, IC, D])
        wsd = sb(ctx, "wsd", [P, D])
        su = sb(ctx, "su", [P, DC])
        sud = sb(ctx, "sud", [P, IC])
        kt = sb(ctx, "kt", [DCTX, 2, 2, L])
        kr = sb(ctx, "kr", [P, 2, 2, DCTX])
        ct = sb(ctx, "ct", [DCTX, 2, 2, S])
        ctd = sb(ctx, "ctd", [DCTX, 2, 2, 2, S])
        hTd = sb(ctx, "hTd", [P, 2, DC, 2, 2, S])
        b1 = sb(ctx, "b1", [P, 2, 2048])
        b2 = sb(ctx, "b2", [P, 2, 2048])
        b3 = sb(ctx, "b3", [P, 2, 2048])
        hT = sb(ctx, "hT", [P, 2, DC, P])
        qT = sb(ctx, "qT", [P, 2, DC, P])
        oT = sb(ctx, "oT", [P, 2, DC, P])
        vb = sb(ctx, "vb", [P, 2, 2 * PAIRS, 2, HD])
        mx = sb(ctx, "mx", [P, 2, 16])
        rs = sb(ctx, "rs", [P, 2, 16])
        s = semaphores(ctx, "w_attn w_ffn ws_in f_prep f_pe f_act vzero "
                       + " ".join(f"{n}{p}" for n in PER_P.split() for p in range(2)), "p2_")
        TURNS = TILES // 2

        def tile(i, p):
            return bass.ds(i * 2 + p, 1)

        def queries(p):
            return b1[0:DCTX, p, :].rearrange("p (b g n) -> p b g n", b=2, n=P)

        def probs0(p):
            return b2[:, p, :].rearrange("p (g l) -> p g l", l=L)

        def probsT0(p, b):
            return b1[:, p, b * 1024:(b + 1) * 1024].rearrange("p (g h s) -> p g h s", h=2, s=S)

        def ctxT(p):
            return b3[:, p, 0:1024].rearrange("p (g n) -> p g n", n=P)

        def keys(p, c, b):
            o = (c * 2 + b) * 512
            return b1[:, p, o:o + 512]

        def probs(p):
            return b2[:, p, 0:1024].rearrange("p (h s) -> p h s", s=S)

        def probsT(p):
            return b3[:, p, 0:1024].rearrange("p (g n) -> p g n", n=P)

        def banks(p, a, n):
            return PS[:, 4 * p + a:4 * p + a + n, :].rearrange("p k n -> p (k n)")

        with nc.Block() as block:
            @block.sync
            def _(sp):
                sp.dma_start(dn[:, :, :], d["ffn_dn"]).then_inc(s["w_ffn"], 16)
                sp.dma_start(b2[:, 0, :], d["ffn_ws"].partition_broadcast(P)).then_inc(s["ws_in"], 16)
                sp.dma_start(ug[:, :, :], d["ffn_ug"]).then_inc(s["ws_in"], 16)
                sp.dma_start(wsd[:, :], d["ffn_wsd"].partition_broadcast(P)).then_inc(s["ws_in"], 16)
                sp.dma_start(su[:, :], d["ffn_su"]).then_inc(s["ws_in"], 16)
                sp.dma_start(sud[:, :], d["ffn_sud"]).then_inc(s["ws_in"], 16)
                sp.dma_start(aw[:, :, :], d["attn_w"]).then_inc(s["w_attn"], 16)
                sp.dma_start(xw[:, :, :], d["xattn_w"]).then_inc(s["w_attn"], 16)
                sp.dma_start(xkv[:, :], d["xattn_kv"]).then_inc(s["w_attn"], 16)

                def load(t, p):
                    sp.dma_start(b1[0:DCTX, p, :], TTd[:, bass.ds(t * 2, 2), :, :].rearrange("p b h s -> p (b h s)")).then_inc(s[f"tt{p}"], 16)
                    sp.dma_start(kt[:, p, :, :], kvT[:, bass.ds(t * 2, 2), :]).then_inc(s[f"tt{p}"], 16)
                    sp.dma_start(kr[:, p, :, :], kvr[:, bass.ds(t * 2, 2), :]).then_inc(s[f"tt{p}"], 16)
                    sp.dma_start(ct[:, p, :, :], cxT[:, bass.ds(t * 2, 2), 0:S]).then_inc(s[f"tt{p}"], 16)
                    for w in range(2):
                        sp.dma_start(ctd[:, p, :, w, :], cxT[:, bass.ds(t * 2, 2), 0:S]).then_inc(s[f"tt{p}"], 16)

                sp.wait_ge(s["f_prep"], 13)
                for p in range(2):
                    load(p, p)
                with sp.Fori(0, TURNS - 1) as i:
                    for p in range(2):
                        sp.wait_ge(s[f"aout{p}"], i * 2 + 2)
                        load(i * 2 + p + 2, p)

            @block.tensor
            def _(pe):
                pe.wait_ge(s["w_ffn"], 16)
                for k in range(4):
                    mm = pe.matmul(PS[:, k, :], C("had"), dn[:, 2 * k:2 * k + 2, :], start=True, stop=True)
                mm.then_inc(s["f_pe"], 1)
                pe.wait_ge(s["w_attn"], 48)
                pe.wait_ge(s["f_prep"], 14)
                pe.wait_ge(s["vzero"], 1)
                for p in range(2):
                    pe.sem_inc(s[f"turned{p}"], 1)

                def turn(i, q, p):
                    norm_turn(pe, i * 4 + q, p, 4 * p, s[f"stats{p}"], s[f"turned{p}"])

                def attention(i, a, p):
                    n = i * 2 + a
                    wq, wo = (aw[:, :, 0:D], aw[:, :, 3 * D:4 * D]) if a == 0 else (xw[:, :, 0:D], xw[:, :, D:2 * D])
                    q0, k0 = PS[:, 4 * p + 2, 0:D], PS[:, 4 * p, D:2 * D]
                    pe.wait_ge(s[f"hT{p}"], i * 3 + a + 2)
                    for c in range(DC):
                        for k in range(DC):
                            pe.matmul(q0[:, c * P:(c + 1) * P], wq[:, k, c * P:(c + 1) * P], hT[:, p, k, :],
                                      start=(k == 0), stop=(k == DC - 1))
                    for c in range(DC):
                        if a == 0:
                            for k in range(DC):
                                pe.matmul(k0[:, c * P:(c + 1) * P], aw[:, k, D + c * P:D + (c + 1) * P], hT[:, p, k, :],
                                          start=(k == 0), stop=(k == DC - 1))
                        else:
                            pe.matmul(k0[:, c * P:(c + 1) * P], xkv[:, c * P:(c + 1) * P], ct[:, p, :, :],
                                      start=True, stop=True)
                    for b in range(2):
                        if a == 0:
                            for k in range(DC):
                                mm = pe.matmul(PS[:, 4 * p + 1, b * D:(b + 1) * D], hTd[:, p, k, b, :, :].rearrange("p w s -> p (w s)"),
                                               aw[:, k, 2 * D:3 * D], start=(k == 0), stop=(k == DC - 1))
                        else:
                            mm = pe.matmul(PS[:, 4 * p + 1, b * D:(b + 1) * D], ctd[:, p, b, :, :].rearrange("p w s -> p (w s)"),
                                           xkv[:, D:2 * D], start=True, stop=True)
                    mm.then_inc(s[f"qkv{p}"], 1)

                def scores(i, a, p):
                    n = i * 2 + a
                    pe.wait_ge(s[f"q{p}"], n + 1)
                    pe.wait_ge(s[f"kb{p}"], n * 4 + 4)
                    for c in range(DC):
                        for b in range(2):
                            mm = pe.matmul(PS[64 * b:64 * b + S, 4 * p + 2 + c, :], qT[:, p, c, b * S:(b + 1) * S],
                                           keys(p, c, b), start=True, stop=True)
                    mm.then_inc(s[f"asc{p}"], 1)

                def probs_turn(i, a, p):
                    n = i * 2 + a
                    pe.wait_ge(s[f"anr{p}"], n * 3 + 3)
                    pe.wait_ge(s[f"vv{p}"], n * 2 + 2)
                    for g in range(PAIRS):
                        mm = pe.transpose(PS[:, 4 * p + g // 4, (g % 4) * P:(g % 4 + 1) * P],
                                          b2[:, p, g * P:(g + 1) * P], C("ident"))
                    mm.then_inc(s[f"atp{p}"], 1)

                def values(i, a, p):
                    n = i * 2 + a
                    pe.wait_ge(s[f"apt{p}"], n + 1)
                    for b in range(2):
                        for g in range(PAIRS):
                            r = 32 * (g % 4)
                            o = (g // 4) * P + b * S
                            mm = pe.matmul(PS[r:r + 32, 4 * p + 2, o:o + S],
                                           vb[:, p, b * PAIRS + g, :, :].rearrange("p h d -> p (h d)"),
                                           probsT(p)[:, g, b * S:(b + 1) * S], start=True, stop=True,
                                           tile_position=(0, r))
                    mm.then_inc(s[f"av{p}"], 1)

                def project(i, a, p):
                    n = i * 2 + a
                    wo = aw[:, :, 3 * D:4 * D] if a == 0 else xw[:, :, D:2 * D]
                    pe.wait_ge(s[f"ot{p}"], n + 1)
                    for k in range(DC):
                        mm = pe.matmul(PS[:, 4 * p + 3, 0:D], oT[:, p, k, :], wo[:, k, :], start=(k == 0), stop=(k == DC - 1))
                    mm.then_inc(s[f"aout{p}"], 1)

                def narrow(i, a):
                    for step in (attention, scores, probs_turn, values, project):
                        for p in range(2):
                            step(i, a, p)

                with pe.Fori(0, TURNS) as i:
                    for p in range(2):
                        pe.wait_ge(s[f"tt{p}"], i * 96 + 96)
                        pe.wait_ge(s[f"hT{p}"], i * 3 + 1)
                        for b in range(2):
                            for g in range(H0 // 2):
                                mm = pe.matmul(PS[:, 4 * p + 2 * b + g // 4, (g % 4) * L:(g % 4 + 1) * L],
                                               queries(p)[:, b, g, :],
                                               kt[:, p, b, :], start=True, stop=True)
                        mm.then_inc(s[f"sc{p}"], 1)
                    for p in range(2):
                        pe.wait_ge(s[f"nr{p}"], i * 3 + 3)
                        for b in range(2):
                            for g in range(H0 // 2):
                                mm = pe.transpose(PS[:, 4 * p + 2 * b + g // 4, (g % 4) * P:(g % 4 + 1) * P],
                                                  probs0(p)[:, b * 8 + g, :], C("ident"))
                            mm.then_inc(s[f"tp{p}"], 1)
                    for p in range(2):
                        for b in range(2):
                            pe.wait_ge(s[f"pt{p}"], i * 2 + b + 1)
                            for h in range(2):
                                mm = pe.matmul(PS[64 * h:64 * h + DCTX, 4 * p + 2 * b, :], kr[:, p, b, :],
                                               probsT0(p, b)[:, :, h, :], start=True, stop=True)
                            mm.then_inc(s[f"cx{p}"], 1)
                    for p in range(2):
                        pe.wait_ge(s[f"ct{p}"], i * 2 + 2)
                        for g in range(H0 // 2):
                            mm = pe.matmul(PS[:, 4 * p + 1, 0:D], ctxT(p)[:, g, :], W2[:, g, :],
                                           start=(g == 0), stop=(g == H0 // 2 - 1))
                        mm.then_inc(s[f"out{p}"], 1)
                    for p in range(2):
                        turn(i, 0, p)
                    narrow(i, 0)
                    for p in range(2):
                        turn(i, 1, p)
                    for p in range(2):
                        pe.wait_ge(s[f"fx{p}"], i + 1)
                        for c in range(DC):
                            pe.matmul(PS[:, 4 * p + 1, c * P:(c + 1) * P], C("had"), hT[:, p, 0, :], start=True, stop=False)
                            mm = pe.matmul(PS[:, 4 * p + 1, c * P:(c + 1) * P], C("nhad" if c else "had"), hT[:, p, 1, :],
                                           start=False, stop=True)
                        mm.then_inc(s[f"fh{p}"], 1)
                    for p in range(2):
                        pe.wait_ge(s[f"fhs{p}"], i + 1)
                        for m in range(2 * IC):
                            for k in range(DC):
                                mm = pe.matmul(PS[:, 4 * p + m // 4, (m % 4) * P:(m % 4 + 1) * P], ug[:, k, m * P:(m + 1) * P],
                                               qT[:, p, k, :], start=(k == 0), stop=(k == DC - 1))
                        mm.then_inc(s[f"ug{p}"], 1)
                    for p in range(2):
                        pe.wait_ge(s[f"fy{p}"], i * 2 + 2)
                        for m in range(IC):
                            mm = pe.matmul(PS[:, 4 * p, 0:D], b3[:, p, m * P:(m + 1) * P], dn[:, m, :],
                                           start=(m == 0), stop=(m == IC - 1))
                        mm.then_inc(s[f"fo{p}"], 1)
                    for p in range(2):
                        turn(i, 2, p)
                    narrow(i, 1)
                    for p in range(2):
                        turn(i, 3, p)

            @block.scalar
            def _(a):
                a.wait_ge(s["f_pe"], 1)
                a.activation(b1[:, 0, :], PS[:, 0:4, :].rearrange("p k n -> p (k n)"), ACT.Copy).then_inc(s["f_act"], 1)
                for p in range(2):
                    a.sem_inc(s[f"hT{p}"], 1)

                def copy_hT(i, q, p):
                    n = i * 4 + q
                    a.wait_ge(s[f"turned{p}"], n + 2)
                    if q == 1:
                        for c in range(DC):
                            x = a.activation(hT[:, p, c, :], PS[:, 4 * p, c * P:(c + 1) * P], ACT.Copy, scale=su[:, c:c + 1])
                        x.then_inc(s[f"fx{p}"], 1)
                    elif q == 3:
                        a.activation(HT[:, :, bass.ds(i * 2 * P + p * P, P)], hT_psum(4 * p), ACT.Copy).then_inc(s[f"hT{p}"], 1)
                    else:
                        if q == 0:
                            for w in range(2):
                                a.activation(hTd[:, p, :, :, w, :].rearrange("p c b s -> p (c b) s"),
                                             PS[:, 4 * p, 0:D].rearrange("p (g s) -> p g s", s=S), ACT.Copy)
                        a.activation(hT[:, p, :, :], hT_psum(4 * p), ACT.Copy).then_inc(s[f"hT{p}"], 1)

                def narrow(i, k):
                    n = i * 2 + k
                    for p in range(2):
                        a.wait_ge(s[f"qkv{p}"], n + 1)
                        a.activation(qT[:, p, :, :], PS[:, 4 * p + 2, 0:D].rearrange("p (c n) -> p c n", c=DC), ACT.Copy).then_inc(s[f"q{p}"], 1)
                        for h in range(2):
                            r = slice(64 * h, 64 * h + S)
                            a.activation(vb[r, p, :, h, :], PS[r, 4 * p + 1, :].rearrange("p (g h d) -> p g h d", h=2, d=HD)[:, :, h, :],
                                         ACT.Copy).then_inc(s[f"vv{p}"], 1)
                    for p in range(2):
                        a.wait_ge(s[f"asm{p}"], n * 3 + 3)
                        a.activation(probs(p), probs(p), ACT.Exp, scale=(1.0 / 8, 1.0 / 4)[k]).then_inc(s[f"aex{p}"], 1)
                    for p in range(2):
                        a.wait_ge(s[f"atp{p}"], n + 1)
                        a.activation(b3[:, p, 0:1024], banks(p, 0, 2), ACT.Copy).then_inc(s[f"apt{p}"], 1)
                    for p in range(2):
                        a.wait_ge(s[f"av{p}"], n + 1)
                        a.activation(oT[:, p, :, :], PS[:, 4 * p + 2, 0:D].rearrange("p (c n) -> p c n", c=DC), ACT.Copy).then_inc(s[f"ot{p}"], 1)

                with a.Fori(0, TURNS) as i:
                    for p in range(2):
                        a.wait_ge(s[f"sm{p}"], i * 2 + 2)
                        a.activation(probs0(p), probs0(p), ACT.Exp).then_inc(s[f"ex{p}"], 1)
                    for p in range(2):
                        for b in range(2):
                            a.wait_ge(s[f"tp{p}"], i * 2 + b + 1)
                            a.activation(b1[:, p, b * 1024:(b + 1) * 1024], banks(p, 2 * b, 2), ACT.Copy).then_inc(s[f"pt{p}"], 1)
                    for p in range(2):
                        for b in range(2):
                            a.wait_ge(s[f"cx{p}"], i * 2 + b + 1)
                            a.activation(ctxT(p)[:, :, b * S:(b + 1) * S], PS[:, 4 * p + 2 * b, :].rearrange("p (g s) -> p g s", s=S),
                                         ACT.Copy).then_inc(s[f"ct{p}"], 1)
                    for p in range(2):
                        copy_hT(i, 0, p)
                    narrow(i, 0)
                    for p in range(2):
                        copy_hT(i, 1, p)
                    for p in range(2):
                        a.wait_ge(s[f"fh{p}"], i + 1)
                        a.activation(qT[:, p, :, :], PS[:, 4 * p + 1, 0:D].rearrange("p (c n) -> p c n", c=DC), ACT.Copy,
                                     scale=D ** -0.5).then_inc(s[f"fhs{p}"], 1)
                    for p in range(2):
                        a.wait_ge(s[f"ug{p}"], i + 1)
                        a.activation(b2[:, p, 0:1024], banks(p, 2, 2), ACT.Tanh, scale=0.5).then_inc(s[f"th{p}"], 1)
                    for p in range(2):
                        copy_hT(i, 2, p)
                    narrow(i, 1)
                    for p in range(2):
                        copy_hT(i, 3, p)

            @block.gpsimd
            def _(g):
                g.memset(vb[:, :, :, :, :], 0.0).then_inc(s["vzero"], 1)
                with g.Fori(0, TURNS) as i:
                    for q in range(4):
                        for p in range(2):
                            norm_root(g, i * 4 + q, p, s[f"stats{p}"], s[f"root{p}"])

            @block.vector
            def _(v):
                prep = s["f_prep"]
                v.wait_ge(s["f_act"], 1)
                src, k = b1[:, 0, :], 0
                for st, dst in ((1, b3[:, 0, :]), (2, b1[:, 1, :]), (4, dn[:, :, :].rearrange("p c n -> p (c n)"))):
                    a0 = src.rearrange("p (g two n) -> p g two n", two=2, n=st * D)
                    o0 = dst.rearrange("p (g two n) -> p g two n", two=2, n=st * D)
                    if k:
                        v.wait_ge(prep, k)
                    v.tensor_tensor(o0[:, :, 0, :], a0[:, :, 0, :], a0[:, :, 1, :], ALU.add).then_inc(prep, 1)
                    v.tensor_tensor(o0[:, :, 1, :], a0[:, :, 0, :], a0[:, :, 1, :], ALU.subtract).then_inc(prep, 1)
                    src, k = dst, k + 2
                v.wait_ge(s["ws_in"], 80)
                for k in range(DC):
                    v.tensor_tensor(ug[:, k, :], ug[:, k, :], b2[:, 0, :], ALU.mult)
                v.tensor_scalar(sud[:, :], sud[:, :], INTER ** -0.5 / 2, None, ALU.mult).then_inc(prep, 1)
                v.wait_ge(prep, 7)
                v.tensor_tensor(dn[:, :, :], dn[:, :, :], each(sud[:, :], D), ALU.mult).then_inc(prep, 1)
                v.wait_ge(prep, 8)
                v.tensor_tensor(dn[:, :, :], dn[:, :, :], over(wsd[:, :], IC), ALU.mult).then_inc(prep, 6)

                def softmax_tail(x, p, sem, n):
                    v.tensor_reduce(rs[:, p, :], x, AX.X, ALU.add).then_inc(sem, 1)
                    v.wait_ge(sem, n * 3 + 1)
                    v.reciprocal(rs[:, p, :], rs[:, p, :]).then_inc(sem, 1)
                    v.wait_ge(sem, n * 3 + 2)
                    v.tensor_tensor(x, x, each(rs[:, p, :], x.shape[2]), ALU.mult).then_inc(sem, 1)

                def residual(i, p, bank, ready, n, done):
                    v.wait_ge(ready, n)
                    v.tensor_tensor(X[:, tile(i, p), :], X[:, tile(i, p), :], PS[:, bank, 0:D].unsqueeze(1), ALU.add).then_inc(done, 1)

                def norm(i, q, done, n):
                    for p in range(2):
                        v.wait_ge(s[f"{done}{p}"], n)
                        v.memset(carrier[:, :], 0.0)
                        norm_stats(v, i, p, s[f"stats{p}"], i * 4 + q)
                    for p in range(2):
                        norm_apply(v, i, p, s[f"stats{p}"], s[f"root{p}"], s[f"turned{p}"], i * 4 + q)

                def narrow(i, a):
                    n = i * 2 + a
                    for p in range(2):
                        v.wait_ge(s[f"qkv{p}"], n + 1)
                        for c in range(DC):
                            for b in range(2):
                                o = D + c * P + b * S
                                v.tensor_tensor(keys(p, c, b).rearrange("p (h s) -> p h s", s=S),
                                                over(PS[:, 4 * p, o:o + S], 8), each(C("head"), S), ALU.mult).then_inc(s[f"kb{p}"], 1)
                    for p in range(2):
                        x = probs(p)
                        sem = s[f"asm{p}"]
                        v.wait_ge(s[f"asc{p}"], n + 1)
                        v.tensor_tensor(x, banks(p, 2, 2).rearrange("p (h s) -> p h s", s=S), over(C("tril" if a == 0 else "neg"), NH),
                                        ALU.mult if a == 0 else ALU.add).then_inc(sem, 1)
                        v.wait_ge(sem, n * 3 + 1)
                        v.tensor_reduce(mx[:, p, :], x, AX.X, ALU.max).then_inc(sem, 1)
                        v.wait_ge(sem, n * 3 + 2)
                        v.tensor_tensor(x, x, each(mx[:, p, :], S), ALU.subtract).then_inc(sem, 1)
                    for p in range(2):
                        v.wait_ge(s[f"aex{p}"], n + 1)
                        softmax_tail(probs(p), p, s[f"anr{p}"], n)
                    for p in range(2):
                        residual(i, p, 4 * p + 3, s[f"aout{p}"], n + 1, s[f"ares{p}"])

                with v.Fori(0, TURNS) as i:
                    for p in range(2):
                        v.wait_ge(s[f"sc{p}"], i + 1)
                        x, sem = banks(p, 0, 4).rearrange("p (g l) -> p g l", l=L), s[f"sm{p}"]
                        v.tensor_reduce(mx[:, p, :], x, AX.X, ALU.max).then_inc(sem, 1)
                        v.wait_ge(sem, i * 2 + 1)
                        v.tensor_tensor(probs0(p), x, each(mx[:, p, :], L), ALU.subtract).then_inc(sem, 1)
                    for p in range(2):
                        v.wait_ge(s[f"ex{p}"], i + 1)
                        softmax_tail(probs0(p), p, s[f"nr{p}"], i)
                    for p in range(2):
                        residual(i, p, 4 * p + 1, s[f"out{p}"], i + 1, s[f"res{p}"])
                    norm(i, 0, "res", i + 1)
                    narrow(i, 0)
                    norm(i, 1, "ares", i * 2 + 1)
                    for p in range(2):
                        v.wait_ge(s[f"th{p}"], i + 1)
                        v.scalar_tensor_tensor(b3[:, p, 0:1024], b2[:, p, 0:1024], 1.0, banks(p, 2, 2), ALU.add, ALU.mult).then_inc(s[f"fy{p}"], 1)
                        v.wait_ge(s[f"fy{p}"], i * 2 + 1)
                        v.tensor_tensor(b3[:, p, 0:1024], b3[:, p, 0:1024], banks(p, 0, 2), ALU.mult).then_inc(s[f"fy{p}"], 1)
                    for p in range(2):
                        residual(i, p, 4 * p, s[f"fo{p}"], i + 1, s[f"fres{p}"])
                    norm(i, 2, "fres", i + 1)
                    narrow(i, 1)
                    norm(i, 3, "ares", i * 2 + 2)


def phase3(nc, d, sb, semaphores, C, over, each, X, HT, PS, carrier):
    TK = B * S
    with ExitStack() as ctx:
        ga = sb(ctx, "ga", [P, TILES, 2 * HV])
        with ExitStack() as c2:
            wab = sb(c2, "wab", [P, DC, 2 * HV])
            al = sb(c2, "al", [P, HV])
            dtb = sb(c2, "dtb", [P, HV])
            ab = sb(c2, "ab", [P, TILES, 2 * HV])
            e = sb(c2, "e", [P, TILES, 2 * HV])
            s = semaphores(c2, "ab_in ab_mm ab_v ab_a")
            av, bv = ab[:, :, 0:HV], ab[:, :, HV:2 * HV]
            ea, eb = e[:, :, 0:HV], e[:, :, HV:2 * HV]
            with nc.Block() as block:
                @block.sync
                def _(sp):
                    sp.dma_start(wab[:, :, :], d["gdn_ab"]).then_inc(s["ab_in"], 16)
                    sp.dma_start(al[:, :], d["gdn_al"].partition_broadcast(P)).then_inc(s["ab_in"], 16)
                    sp.dma_start(dtb[:, :], d["gdn_dt"].partition_broadcast(P)).then_inc(s["ab_in"], 16)

                @block.tensor
                def _(pe):
                    pe.wait_ge(s["ab_in"], 48)
                    for n in range(TILES):
                        for k in range(DC):
                            mm = pe.matmul(PS[:, 0, n * 2 * HV:(n + 1) * 2 * HV], HT[:, k, n * P:(n + 1) * P], wab[:, k, :],
                                           start=(k == 0), stop=(k == DC - 1))
                    mm.then_inc(s["ab_mm"], 1)

                @block.vector
                def _(v):
                    ps = PS[:, 0, :].rearrange("p (n h) -> p n h", n=TILES)
                    v.wait_ge(s["ab_mm"], 1)
                    v.tensor_tensor(av, ps[:, :, 0:HV], over(dtb[:, :], TILES), ALU.add).then_inc(s["ab_v"], 1)
                    v.tensor_scalar(bv, ps[:, :, HV:2 * HV], -1.0, 80.0, ALU.mult, ALU.min).then_inc(s["ab_v"], 1)
                    v.wait_ge(s["ab_a"], 1)
                    v.tensor_scalar(eb, eb, 1.0, None, ALU.add).then_inc(s["ab_v"], 1)
                    v.wait_ge(s["ab_v"], 3)
                    v.reciprocal(ga[:, :, HV:2 * HV], eb)
                    v.wait_ge(s["ab_a"], 5)
                    v.tensor_scalar(av, av, 0.0, None, ALU.max).then_inc(s["ab_v"], 1)
                    v.wait_ge(s["ab_v"], 4)
                    v.tensor_tensor(av, av, ea, ALU.add).then_inc(s["ab_v"], 1)
                    v.tensor_scalar(al[:, :], al[:, :], -1.0, None, ALU.mult).then_inc(s["ab_v"], 1)
                    v.wait_ge(s["ab_v"], 6)
                    v.tensor_tensor(ga[:, :, 0:HV], av, over(al[:, :], TILES), ALU.mult)

                @block.scalar
                def _(a):
                    a.wait_ge(s["ab_v"], 2)
                    a.activation(eb, bv, ACT.Exp).then_inc(s["ab_a"], 1)
                    a.activation(al[:, :], al[:, :], ACT.Exp).then_inc(s["ab_a"], 1)
                    a.activation(ea, av, ACT.Abs).then_inc(s["ab_a"], 1)
                    a.wait_ge(s["ab_a"], 3)
                    a.activation(ea, ea, ACT.Exp, scale=-1.0).then_inc(s["ab_a"], 1)
                    a.wait_ge(s["ab_a"], 4)
                    a.activation(ea, ea, ACT.Ln, bias=1.0).then_inc(s["ab_a"], 1)

        NW = DC * 4 * DK + DC * 2 * DK
        wp = sb(ctx, "wp", [P, NW])
        wc = sb(ctx, "wc", [P, 16])
        wo = sb(ctx, "wo", [P, 2, D])
        nw = sb(ctx, "nw", [P, 1])
        gj = sb(ctx, "gj", [P, TILES, 4])
        gm = sb(ctx, "gm", [P, 2, TILES, S])
        E = sb(ctx, "E", [P, 2, TILES, S])
        Et = sb(ctx, "Et", [P, 2, TILES, S])
        acc = sb(ctx, "acc", [P, 2, TK])
        th = sb(ctx, "th", [P, 2, TK])
        y = sb(ctx, "y", [P, 4, TK])
        sq = sb(ctx, "sq", [P, 2, TK])
        z2 = sb(ctx, "z2", [P, 2, TILES, DK])
        nm = sb(ctx, "nm", [P, 2 * TILES])
        rr = sb(ctx, "rr", [P, 2 * TILES])
        rq2 = sb(ctx, "rq2", [P, TILES])
        bk = sb(ctx, "bk", [P, 2, TILES])
        dd = sb(ctx, "dd", [P, 2, TILES])
        A = sb(ctx, "A", [P, 2, TILES, 2, S])
        AT = sb(ctx, "AT", [P, 2, TILES, P])
        T = sb(ctx, "T", [P, 2, TILES, 2, S])
        TT = sb(ctx, "TT", [P, 2, TILES, P])
        PT = sb(ctx, "PT", [P, 2, TILES, P])
        Xs = sb(ctx, "Xs", [P, 2, TILES, S])
        V = sb(ctx, "V", [P, 2, TILES, DK])
        dl = sb(ctx, "dl", [P, 2, TILES, DK])
        ms = sb(ctx, "ms", [P, 2, TILES])
        s = semaphores(ctx, "win cin oin nin z zt z2 pj tap conv th y sq ss kk gj gm dps e et ed nm rr av pd vt vs at ats "
                            "pt pts ti tt tts x xs yy tu dl ds u us ms fz og ogt ogs wo xa wof zero", "p3_")

        def wide(b0):
            return PS[:, b0:b0 + 2, :].rearrange("p k n -> p (k n)")

        def turned(hv):
            return 6 if hv == 0 else 2

        def twice(ap):
            return ap.unsqueeze(2).broadcast_to([P, TILES, 2, S])

        def blocks(ap, b):
            return ap[64 * b:64 * b + S, :, 64 * b:64 * b + S]

        def bank(k):
            return PS[:, k, :].rearrange("p (n s) -> p n s", s=S)

        HEADS = HK
        with nc.Block() as block:
            @block.sync
            def _(sp):
                def load(j):
                    w = d["gdn_w"][bass.ds(j, 1), :, :].rearrange("a p n -> (a p) n")
                    sp.dma_start(wp[:, :], w[:, 0:NW]).then_inc(s["win"], 16)
                    return w

                def load_rest(j):
                    w = d["gdn_w"][bass.ds(j, 1), :, :].rearrange("a p n -> (a p) n")
                    sp.dma_start(wc[:, :], w[:, NW + 2 * D:]).then_inc(s["cin"], 16)

                def load_out(j):
                    w = d["gdn_w"][bass.ds(j, 1), :, :].rearrange("a p n -> (a p) n")
                    sp.dma_start(wo[:, :, :].rearrange("p c n -> p (c n)"), w[:, NW:NW + 2 * D]).then_inc(s["oin"], 16)

                sp.dma_start(nw[:, :], d["gdn_nw"]).then_inc(s["nin"], 16)
                load(0)
                load_rest(0)
                load_out(0)
                with sp.Fori(0, HEADS - 1) as j:
                    sp.wait_ge(s["pj"], j * 4 + 4)
                    load(j + 1)
                    sp.wait_ge(s["conv"], j * 24 + 24 + 12)
                    load_rest(j + 1)
                    sp.wait_ge(s["wo"], j + 1)
                    load_out(j + 1)

            @block.tensor
            def _(pe):
                pe.wait_ge(s["zero"], 3)
                with pe.Fori(0, HEADS) as j:
                    pe.wait_ge(s["win"], j * 16 + 16)
                    pe.wait_ge(s["xa"], j + 1)
                    for n in range(TILES):
                        for k in range(DC):
                            o = DC * 4 * DK + k * 2 * DK
                            mm = pe.matmul(PS[:, 4 + n // 2, (n % 2) * 256:(n % 2 + 1) * 256], HT[:, k, n * P:(n + 1) * P],
                                           wp[:, o:o + 2 * DK], start=(k == 0), stop=(k == DC - 1))
                    mm.then_inc(s["z"], 1)
                    for c in range(4):
                        if c < 2:
                            pe.wait_ge(s["ogs"], j * 2 + 2)
                        pe.wait_ge(s["conv"], j * 24 + c * 6 + 6)
                        for f in range(2):
                            for k in range(DC):
                                o = k * 4 * DK + c * DK
                                mm = pe.matmul(PS[:, 2 * (c % 2) + f, :], wp[:, o:o + DK], HT[:, k, f * 512:(f + 1) * 512],
                                               start=(k == 0), stop=(k == DC - 1))
                        mm.then_inc(s["pj"], 1)
                    pe.wait_ge(s["z2"], j + 1)
                    for c in range(2):
                        pe.wait_ge(s["y"], j * 4 + c + 1 + 2)
                        for n in range(TILES):
                            for b in range(2):
                                o = n * P + b * S
                                mm = pe.matmul(PS[64 * b:64 * b + S, 4 + c, n * S:(n + 1) * S], y[:, c, o:o + S], y[:, 0, o:o + S],
                                               start=True, stop=True)
                        mm.then_inc(s["kk"], 1)
                    for hv in range(2):
                        pe.wait_ge(s["gm"], j * 2 + hv + 1)
                        pe.matmul(PS[:, 6 + hv, :], C("cumsum"), gm[:, hv, :, :].rearrange("p n s -> p (n s)"),
                                  start=True, stop=True).then_inc(s["dps"], 1)
                    pe.wait_ge(s["sq"], j * 2 + 2)
                    pe.wait_ge(s["e"], j * 2 + 1)
                    for c in range(2):
                        for n in range(TILES):
                            mm = pe.matmul(PS[:, 6, c * TILES + n:c * TILES + n + 1], sq[:, c, n * P:(n + 1) * P], C("ones"),
                                           start=True, stop=True)
                    mm.then_inc(s["ss"], 1)
                    for hv in range(2):
                        pe.wait_ge(s["y"], j * 4 + 3 + hv + 2)
                        for n in range(TILES):
                            mm = pe.transpose(PS[:, 2 * hv + n // 4, (n % 4) * P:(n % 4 + 1) * P], y[:, 2 + hv, n * P:(n + 1) * P], C("ident"))
                        mm.then_inc(s["vt"], 1)

                    def turn(src, hv):
                        for n in range(TILES):
                            mm = pe.transpose(PS[:, turned(hv) + n // 4, (n % 4) * P:(n % 4 + 1) * P],
                                              src[:, hv, n, :, :].rearrange("p w s -> p (w s)"), C("ident"))
                        return mm

                    for hv in range(2):
                        pe.wait_ge(s["av"], j * 2 + hv + 1)
                        pe.wait_ge(s["e"], j * 2 + 2)
                        pe.wait_ge(s["vs"], j * 2 + 2)
                        turn(A, hv).then_inc(s["at"], 1)
                    for hv in range(2):
                        pe.wait_ge(s["pd"], j * 2 + hv + 1)
                        pe.wait_ge(s["ats"], j * 4 + hv * 2 + 2)
                        turn(A, hv).then_inc(s["pt"], 1)
                    for k in range(1, LEVELS):
                        for hv in range(2):
                            if k == 1:
                                pe.wait_ge(s["ti"], j * 4 + hv * 2 + 2)
                                pe.wait_ge(s["pts"], j * 4 + hv * 2 + 2)
                            else:
                                pe.wait_ge(s["tu"], j * 10 + (k - 2) * 2 + hv + 1)
                            turn(T, hv).then_inc(s["tt"], 1)
                            for n in range(TILES):
                                mm = pe.matmul(PS[:, 4 + hv, n * S:(n + 1) * S], AT[:, hv, n, :], T[:, hv, n, 0, :], start=True, stop=True)
                            mm.then_inc(s["x"], 1)
                        for hv in range(2):
                            pe.wait_ge(s["xs"], j * 10 + (k - 1) * 2 + hv + 1)
                            pe.wait_ge(s["tts"], j * 24 + (k - 1) * 4 + hv * 2 + 2)
                            for n in range(TILES):
                                mm = pe.matmul(PS[:, 4 + hv, n * S:(n + 1) * S], TT[:, hv, n, :], Xs[:, hv, n, :], start=True, stop=True)
                            mm.then_inc(s["yy"], 1)
                    for hv in range(2):
                        pe.wait_ge(s["tu"], j * 10 + 8 + hv + 1)
                        turn(T, hv).then_inc(s["tt"], 1)

                    def apply(lhs, rhs, hv):
                        for n in range(TILES):
                            mm = pe.matmul(PS[:, 2 * hv + n // 4, (n % 4) * P:(n % 4 + 1) * P], lhs[:, hv, n, :], rhs[:, hv, n, :],
                                           start=True, stop=True)
                        return mm

                    for hv in range(2):
                        pe.wait_ge(s["tts"], j * 24 + 20 + hv * 2 + 2)
                        apply(TT, V, hv).then_inc(s["dl"], 1)
                    for hv in range(2):
                        pe.wait_ge(s["ds"], j * 2 + hv + 1)
                        apply(PT, dl, hv).then_inc(s["u"], 1)
                    for hv in range(2):
                        pe.wait_ge(s["og"], j * 2 + hv + 1)
                        for n in range(TILES):
                            mm = pe.transpose(PS[:, 2 * hv + n // 4, (n % 4) * P:(n % 4 + 1) * P], dl[:, hv, n, :], C("ident"))
                        mm.then_inc(s["ogt"], 1)
                    pe.wait_ge(s["ogs"], j * 2 + 4)
                    pe.wait_ge(s["wof"], j + 1)
                    for n in range(TILES):
                        for hv in range(2):
                            mm = pe.matmul(PS[:, 4 + n // 2, (n % 2) * D:(n % 2 + 1) * D], V[:, hv, n, :], wo[:, hv, :],
                                           start=(hv == 0), stop=(hv == 1))
                    mm.then_inc(s["wo"], 1)

            @block.scalar
            def _(a):
                a.sem_inc(s["ogs"], 2)
                with a.Fori(0, HEADS) as j:
                    def taps(c):
                        a.wait_ge(s["pj"], j * 4 + c + 1)
                        a.wait_ge(s["y"], j * 4 + c + 1)
                        if c == 0:
                            a.wait_ge(s["cin"], j * 16 + 16)
                        for f in range(2):
                            a.activation(acc[:, c % 2, f * 512:(f + 1) * 512], PS[:, 2 * (c % 2) + f, :], ACT.Copy,
                                         scale=wc[:, 4 * c + 3:4 * c + 4]).then_inc(s["tap"], 1)

                    def tanh(c):
                        a.wait_ge(s["conv"], j * 24 + c * 6 + 6 + 12)
                        a.activation(th[:, c % 2, :], acc[:, c % 2, :], ACT.Tanh, scale=0.5).then_inc(s["th"], 1)

                    def square(c):
                        a.wait_ge(s["y"], j * 4 + c + 1 + 2)
                        a.activation(sq[:, c, :], y[:, c, :], ACT.Square).then_inc(s["sq"], 1)

                    taps(0)
                    a.wait_ge(s["z"], j + 1)
                    for hv in range(2):
                        a.activation(V[:, hv, :, :], PS[:, 4:8, :].rearrange("p k (w h c) -> p (k w) h c", w=2, h=2)[:, :, hv, :],
                                     ACT.Tanh, scale=0.5).then_inc(s["zt"], 1)
                    taps(1)
                    tanh(0)
                    taps(2)
                    tanh(1)
                    square(0)
                    taps(3)
                    tanh(2)
                    square(1)
                    for hv in range(2):
                        a.wait_ge(s["dps"], j * 2 + hv + 1)
                        a.activation(E[:, hv, :, :], bank(6 + hv), ACT.Exp).then_inc(s["e"], 1)
                    tanh(3)

                    def split(dst, hv, done):
                        for b in range(2):
                            a.activation(blocks(dst[:, hv, :, :], b),
                                         blocks(wide(turned(hv)).rearrange("p (n t) -> p n t", t=P), b), ACT.Copy).then_inc(done, 1)

                    for hv in range(2):
                        a.wait_ge(s["at"], j * 2 + hv + 1)
                        split(AT, hv, s["ats"])
                    for hv in range(2):
                        a.wait_ge(s["pt"], j * 2 + hv + 1)
                        split(PT, hv, s["pts"])
                    for k in range(1, LEVELS + 1):
                        for hv in range(2):
                            a.wait_ge(s["tt"], j * 12 + (k - 1) * 2 + hv + 1)
                            split(TT, hv, s["tts"])
                    for hv in range(2):
                        a.wait_ge(s["dl"], j * 2 + hv + 1)
                        a.activation(dl[:, hv, :, :].rearrange("p n c -> p (n c)"), wide(2 * hv), ACT.Copy).then_inc(s["ds"], 1)
                    for hv in range(2):
                        a.wait_ge(s["u"], j * 2 + hv + 1)
                        a.activation(sq[:, hv, :], wide(2 * hv), ACT.Square).then_inc(s["us"], 1)
                    for hv in range(2):
                        a.wait_ge(s["ogt"], j * 2 + hv + 1)
                        a.activation(V[:, hv, :, :].rearrange("p n c -> p (n c)"), wide(2 * hv), ACT.Copy).then_inc(s["ogs"], 1)

            @block.gpsimd
            def _(g):
                for m in (AT, TT, PT):
                    g.memset(m[:, :, :, :], 0.0).then_inc(s["zero"], 1)
                with g.Fori(0, HEADS) as j:
                    for hv in range(2):
                        g.wait_ge(s["gj"], j * 2 + 2)
                        g.tensor_tensor(gm[:, hv, :, :], over(C("strict"), TILES), each(gj[:, :, hv], S), ALU.mult).then_inc(s["gm"], 1)
                    for hv in range(2):
                        g.wait_ge(s["e"], j * 2 + hv + 1)
                        g.tensor_tensor(Et[:, hv, :, :], E[:, hv, :, :], over(C("tril"), TILES), ALU.mult).then_inc(s["et"], 1)
                    g.wait_ge(s["nm"], j + 1)
                    g.tensor_tensor(rr[:, :], nm[:, :], C("mhalf")[:, 0:2 * TILES], ALU.pow).then_inc(s["rr"], 1)
                    g.wait_ge(s["rr"], j * 6 + 1)
                    for hv in range(2):
                        g.tensor_tensor(bk[:, hv, :], gj[:, :, 2 + hv], rr[:, 0:TILES], ALU.mult).then_inc(s["rr"], 1)
                    g.tensor_tensor(rq2[:, :], rr[:, TILES:2 * TILES], rr[:, TILES:2 * TILES], ALU.mult).then_inc(s["rr"], 1)
                    for hv in range(2):
                        g.wait_ge(s["rr"], j * 6 + 2 + hv)
                        g.tensor_tensor(dd[:, hv, :], bk[:, hv, :], rr[:, 0:TILES], ALU.mult).then_inc(s["rr"], 1)
                    for hv in range(2):
                        g.wait_ge(s["rr"], j * 6 + 5 + hv)
                        g.tensor_tensor(E[:, hv, :, :], E[:, hv, :, :], each(dd[:, hv, :], S), ALU.mult).then_inc(s["ed"], 1)
                    for hv in range(2):
                        g.wait_ge(s["ms"], j * 6 + hv * 3 + 3)
                        g.tensor_tensor(ms[:, hv, :], ms[:, hv, :], C("mhalf")[:, 0:TILES], ALU.pow).then_inc(s["fz"], 1)
                        g.wait_ge(s["fz"], j * 6 + hv * 3 + 1)
                        g.tensor_tensor(ms[:, hv, :], ms[:, hv, :], rr[:, TILES:2 * TILES], ALU.mult).then_inc(s["fz"], 1)
                        g.wait_ge(s["fz"], j * 6 + hv * 3 + 2)
                        g.tensor_tensor(z2[:, hv, :, :], z2[:, hv, :, :], each(ms[:, hv, :], DK), ALU.mult).then_inc(s["fz"], 1)

            @block.vector
            def _(v):
                v.sem_inc(s["conv"], 12)
                v.sem_inc(s["y"], 2)
                v.sem_inc(s["xa"], 1)
                v.wait_ge(s["nin"], 16)
                with v.Fori(0, HEADS) as j:
                    v.tensor_copy(gj[:, :, 0:2], ga[:, :, bass.ds(j * 2, 2)]).then_inc(s["gj"], 1)
                    v.tensor_copy(gj[:, :, 2:4], ga[:, :, bass.ds(j * 2 + HV, 2)]).then_inc(s["gj"], 1)
                    v.wait_ge(s["oin"], j * 16 + 16)
                    v.tensor_scalar(wo[:, :, :], wo[:, :, :], nw[:, :], DK ** -0.5 / 4, ALU.mult, ALU.mult).then_inc(s["wof"], 1)

                    def conv(c):
                        for k in range(3):
                            for f in range(2):
                                sh = k + 1
                                a0 = acc[:, c % 2, f * 512:(f + 1) * 512].rearrange("p (b s) -> p b s", s=S)[:, :, sh:S]
                                p0 = PS[:, 2 * (c % 2) + f, :].rearrange("p (b s) -> p b s", s=S)[:, :, 0:S - sh]
                                if k == 0:
                                    v.wait_ge(s["tap"], j * 8 + c * 2 + f + 1)
                                else:
                                    v.wait_ge(s["conv"], j * 24 + c * 6 + (k - 1) * 2 + f + 1 + 12)
                                v.scalar_tensor_tensor(a0, p0, wc[:, 4 * c + 2 - k:4 * c + 3 - k], a0, ALU.mult, ALU.add).then_inc(s["conv"], 1)

                    def silu(c):
                        v.wait_ge(s["th"], j * 4 + c + 1)
                        v.scalar_tensor_tensor(y[:, c, :], th[:, c % 2, :], 1.0, acc[:, c % 2, :], ALU.add, ALU.mult).then_inc(s["y"], 1)

                    conv(0)
                    conv(1)
                    v.wait_ge(s["zt"], j * 2 + 2)
                    for hv in range(2):
                        x = v.scalar_tensor_tensor(z2[:, hv, :, :].rearrange("p n c -> p n c"), V[:, hv, :, :], 1.0,
                                                   PS[:, 4:8, :].rearrange("p k (w h c) -> p (k w) h c", w=2, h=2)[:, :, hv, :],
                                                   ALU.add, ALU.mult)
                    x.then_inc(s["z2"], 1)
                    silu(0)
                    conv(2)
                    silu(1)
                    conv(3)
                    silu(2)
                    silu(3)
                    v.wait_ge(s["ss"], j + 1)
                    v.tensor_scalar(nm[:, :], PS[:, 6, 0:2 * TILES], 4e-12, None, ALU.max).then_inc(s["nm"], 1)
                    for hv in range(2):
                        v.wait_ge(s["vt"], j * 2 + hv + 1)
                        v.wait_ge(s["rr"], j * 6 + 3)
                        v.tensor_tensor(V[:, hv, :, :], wide(2 * hv).rearrange("p (n c) -> p n c", c=DK), each(bk[:, hv, :], DK),
                                        ALU.mult).then_inc(s["vs"], 1)
                    for hv in range(2):
                        v.wait_ge(s["ed"], j * 2 + hv + 1)
                        v.wait_ge(s["kk"], j * 2 + 1)
                        v.tensor_tensor(A[:, hv, :, :, :], twice(bank(4)), twice(E[:, hv, :, :]), ALU.mult).then_inc(s["av"], 1)
                    for hv in range(2):
                        v.wait_ge(s["av"], j * 2 + hv + 1)
                        v.tensor_tensor(Xs[:, hv, :, :], A[:, hv, :, 0, :], over(C("lvl0"), TILES), ALU.mult).then_inc(s["ti"], 1)
                        v.wait_ge(s["ti"], j * 4 + hv * 2 + 1)
                        v.tensor_tensor(T[:, hv, :, :, :], C("eye").unsqueeze(1).unsqueeze(1).broadcast_to([P, TILES, 2, S]),
                                        twice(Xs[:, hv, :, :]), ALU.subtract).then_inc(s["ti"], 1)
                    for hv in range(2):
                        v.wait_ge(s["at"], j * 2 + hv + 1)
                        v.wait_ge(s["et"], j * 2 + hv + 1)
                        v.wait_ge(s["kk"], j * 2 + 2)
                        v.tensor_tensor(A[:, hv, :, :, :], twice(bank(5)), twice(Et[:, hv, :, :]), ALU.mult).then_inc(s["pd"], 1)
                    for k in range(1, LEVELS):
                        for hv in range(2):
                            v.wait_ge(s["x"], j * 10 + (k - 1) * 2 + hv + 1)
                            v.tensor_tensor(Xs[:, hv, :, :], bank(4 + hv), over(C(f"lvl{k}"), TILES), ALU.mult).then_inc(s["xs"], 1)
                        for hv in range(2):
                            v.wait_ge(s["yy"], j * 10 + (k - 1) * 2 + hv + 1)
                            v.tensor_tensor(T[:, hv, :, :, :], T[:, hv, :, :, :], twice(bank(4 + hv)), ALU.subtract).then_inc(s["tu"], 1)
                    for hv in range(2):
                        v.wait_ge(s["us"], j * 2 + hv + 1)
                        v.tensor_reduce(ms[:, hv, :], sq[:, hv, :].rearrange("p (n c) -> p n c", c=DK), AX.X, ALU.add).then_inc(s["ms"], 1)
                        v.wait_ge(s["ms"], j * 6 + hv * 3 + 1)
                        v.tensor_tensor(ms[:, hv, :], ms[:, hv, :], rq2[:, :], ALU.mult).then_inc(s["ms"], 1)
                        v.wait_ge(s["ms"], j * 6 + hv * 3 + 2)
                        v.tensor_scalar(ms[:, hv, :], ms[:, hv, :], 1.0 / (4 * DK * DK), 1e-6, ALU.mult, ALU.add).then_inc(s["ms"], 1)
                    for hv in range(2):
                        v.wait_ge(s["fz"], j * 6 + hv * 3 + 3)
                        v.tensor_tensor(dl[:, hv, :, :].rearrange("p n c -> p (n c)"), wide(2 * hv),
                                        z2[:, hv, :, :].rearrange("p n c -> p (n c)"), ALU.mult).then_inc(s["og"], 1)
                    v.wait_ge(s["wo"], j + 1)
                    v.tensor_tensor(X[:, :, :], X[:, :, :], PS[:, 4:8, :].rearrange("p k (w c) -> p (k w) c", w=2), ALU.add).then_inc(s["xa"], 1)


def phase4(nc, d, sb, semaphores, C, over, each, X, PS, carrier, norm_stats, norm_root, norm_apply, norm_turn, hT_psum):
    W = NE * EI
    with ExitStack() as ctx:
        wr = sb(ctx, "w_router", [P, DC, NE])
        wg = sb(ctx, "wg", [P, DC, W])
        wu = sb(ctx, "wu", [P, DC, W])
        wd = sb(ctx, "wd", [P, MC, D])
        hT = sb(ctx, "hT4", [P, 2, DC, P])
        th = sb(ctx, "th4", [P, 2, 2, 512])
        act = sb(ctx, "act", [P, 2, W])
        acT = sb(ctx, "acT", [P, 2, W])
        lg = sb(ctx, "lg", [P, 2, NE])
        lm = sb(ctx, "lm", [P, 2, 1])
        top = sb(ctx, "top", [P, 2, TOPK])
        rep = sb(ctx, "rep", [P, 2, NE])
        rw = sb(ctx, "rw", [P, 2, NE])
        names = "stats root turned hT lgt le rt gu th y ht aT dn res"
        s = semaphores(ctx, "wsm wup wdn " + " ".join(f"{n}{p}" for n in names.split() for p in range(2)), "p4_")
        with nc.Block() as block:
            @block.sync
            def _(sp):
                sp.dma_start(wr[:, :, :], d["moe_gate"]).then_inc(s["wsm"], 16)
                sp.dma_start(wg[:, :, :], d["moe_g"]).then_inc(s["wup"], 16)
                sp.dma_start(wu[:, :, :], d["moe_u"]).then_inc(s["wup"], 16)
                sp.dma_start(wd[:, :, :], d["moe_d"]).then_inc(s["wdn"], 16)

            @block.tensor
            def _(pe):
                for p in range(2):
                    pe.sem_inc(s[f"turned{p}"], 1)
                pe.wait_ge(s["wsm"], 16)
                with pe.Fori(0, TILES // 2) as i:
                    for p in range(2):
                        pe.wait_ge(s[f"res{p}"], i + 1)
                        norm_turn(pe, i, p, 4 * p, s[f"stats{p}"], s[f"turned{p}"])
                    for p in range(2):
                        pe.wait_ge(s[f"hT{p}"], i + 1)
                        for k in range(DC):
                            mm = pe.matmul(PS[:, 4 * p + 3, 0:NE], hT[:, p, k, :], wr[:, k, :], start=(k == 0), stop=(k == DC - 1))
                        mm.then_inc(s[f"lgt{p}"], 1)
                    pe.wait_ge(s["wup"], 32)
                    for p in range(2):
                        pe.wait_ge(s[f"rt{p}"], i * 6 + 2)
                        for m in range(MB):
                            pe.wait_ge(s[f"y{p}"], i * (2 * MB + 1) + 2 * m + 2)
                            for w, o in ((wg, 0), (wu, 1)):
                                for k in range(DC):
                                    mm = pe.matmul(PS[:, 4 * p + 2 * (m % 2) + o, :], hT[:, p, k, :], w[:, k, m * 512:(m + 1) * 512],
                                                   start=(k == 0), stop=(k == DC - 1))
                            mm.then_inc(s[f"gu{p}"], 1)
                    pe.wait_ge(s["wdn"], 16)
                    for p in range(2):
                        pe.wait_ge(s[f"y{p}"], (i + 1) * (2 * MB + 1) + 4)
                        for m in range(MB + 1):
                            if m < MB:
                                pe.wait_ge(s[f"aT{p}"], i * MB + m + 1)
                                for q in range(4):
                                    c = m * 4 + q
                                    mm = pe.transpose(PS[:, 4 * p + m % 2, q * P:(q + 1) * P], act[:, p, c * P:(c + 1) * P], C("ident"))
                                mm.then_inc(s[f"ht{p}"], 1)
                            if m > 0:
                                pe.wait_ge(s[f"aT{p}"], i * MB + m + 2)
                                for q in range(4):
                                    c = (m - 1) * 4 + q
                                    mm = pe.matmul(PS[:, 4 * p + 2, 0:D], acT[:, p, c * P:(c + 1) * P], wd[:, c, :],
                                                   start=(c == 0), stop=(c == MC - 1))
                        mm.then_inc(s[f"dn{p}"], 1)

            @block.scalar
            def _(a):
                for p in range(2):
                    a.sem_inc(s[f"aT{p}"], 2)
                with a.Fori(0, TILES // 2) as i:
                    for p in range(2):
                        a.wait_ge(s[f"turned{p}"], i + 2)
                        a.activation(hT[:, p, :, :], hT_psum(4 * p), ACT.Copy).then_inc(s[f"hT{p}"], 1)
                    for p in range(2):
                        a.wait_ge(s[f"rt{p}"], i * 6 + 2)
                        a.activation(lg[:, p, :], lg[:, p, :], ACT.Exp).then_inc(s[f"le{p}"], 1)
                    for p in range(2):
                        for m in range(MB):
                            a.wait_ge(s[f"gu{p}"], i * MB + m + 1)
                            a.activation(th[:, p, m % 2, :], PS[:, 4 * p + 2 * (m % 2), :], ACT.Tanh, scale=0.5).then_inc(s[f"th{p}"], 1)
                    for p in range(2):
                        for m in range(MB):
                            a.wait_ge(s[f"ht{p}"], i * MB + m + 1)
                            a.activation(acT[:, p, m * 512:(m + 1) * 512], PS[:, 4 * p + m % 2, :], ACT.Copy).then_inc(s[f"aT{p}"], 1)

            @block.gpsimd
            def _(g):
                with g.Fori(0, TILES // 2) as i:
                    for p in range(2):
                        norm_root(g, i, p, s[f"stats{p}"], s[f"root{p}"])

            @block.vector
            def _(v):
                for p in range(2):
                    v.sem_inc(s[f"res{p}"], 1)
                    v.sem_inc(s[f"y{p}"], 4)
                with v.Fori(0, TILES // 2) as i:
                    for p in range(2):
                        norm_stats(v, i, p, s[f"stats{p}"], i)
                    for p in range(2):
                        norm_apply(v, i, p, s[f"stats{p}"], s[f"root{p}"], s[f"turned{p}"], i)
                    for p in range(2):
                        rt = s[f"rt{p}"]
                        v.wait_ge(s[f"lgt{p}"], i + 1)
                        v.tensor_reduce(lm[:, p, :], PS[:, 4 * p + 3, 0:NE], AX.X, ALU.max).then_inc(rt, 1)
                        v.wait_ge(rt, i * 6 + 1)
                        v.tensor_scalar(lg[:, p, :], PS[:, 4 * p + 3, 0:NE], lm[:, p, :], None, ALU.subtract).then_inc(rt, 1)
                    for p in range(2):
                        rt = s[f"rt{p}"]
                        v.wait_ge(s[f"le{p}"], i + 1)
                        v.memset(carrier[:, :], 0.0)
                        v.max(top[:, p, :], lg[:, p, :]).then_inc(rt, 1)
                        v.wait_ge(rt, i * 6 + 3)
                        v.memset(carrier[:, :], 0.0)
                        v.match_replace(rep[:, p, :], top[:, p, :], lg[:, p, :], -1.0).then_inc(rt, 1)
                        v.tensor_reduce(lm[:, p, :], top[:, p, :], AX.X, ALU.add).then_inc(rt, 1)
                        v.wait_ge(rt, i * 6 + 4)
                        v.scalar_tensor_tensor(rw[:, p, :], rep[:, p, :], 0.0, lg[:, p, :], ALU.is_lt, ALU.mult)
                        v.wait_ge(rt, i * 6 + 5)
                        v.reciprocal(lm[:, p, :], lm[:, p, :]).then_inc(rt, 1)
                        v.wait_ge(rt, i * 6 + 6)
                        v.tensor_scalar(rw[:, p, :], rw[:, p, :], lm[:, p, :], 0.5, ALU.mult, ALU.mult)
                    for p in range(2):
                        yy = s[f"y{p}"]
                        y0 = i * (2 * MB + 1) + 4
                        for m in range(MB):
                            out = act[:, p, m * 512:(m + 1) * 512]
                            v.wait_ge(s[f"th{p}"], i * MB + m + 1)
                            v.scalar_tensor_tensor(out, th[:, p, m % 2, :], 1.0, PS[:, 4 * p + 2 * (m % 2), :], ALU.add, ALU.mult).then_inc(yy, 1)
                            v.wait_ge(yy, y0 + 2 * m + 1)
                            v.tensor_tensor(out, out, PS[:, 4 * p + 2 * (m % 2) + 1, :], ALU.mult).then_inc(yy, 1)
                        v.wait_ge(yy, y0 + 2 * MB)
                        x = act[:, p, :].rearrange("p (e i) -> p e i", i=EI)
                        v.tensor_tensor(x, x, each(rw[:, p, :], EI), ALU.mult).then_inc(yy, 1)
                    for p in range(2):
                        v.wait_ge(s[f"dn{p}"], i + 1)
                        t = bass.ds(i * 2 + p, 1)
                        v.tensor_tensor(X[:, t, :], X[:, t, :], PS[:, 4 * p + 2, 0:D].unsqueeze(1), ALU.add).then_inc(s[f"res{p}"], 1)




def layouts(i):
    def T(a):
        return np.ascontiguousarray(a)
    g = {k: np.asarray(v) for k, v in i.items()}
    n = {"consts": CONSTS, "x": g["x"]}
    ctx = g["ctx_512"]
    rolled = np.concatenate([ctx[..., DCTX // 2:], ctx[..., :DCTX // 2]], axis=-1)
    n["ctx"], n["ctx_rolled"] = T(ctx.transpose(1, 0, 2)), T(rolled.transpose(1, 0, 2))
    n["ctxT"], n["ctxT_rolled"] = T(ctx.transpose(2, 0, 1)), T(rolled.transpose(2, 0, 1))
    n["l0x_k"] = np.concatenate([g["L0_xattn_Wq"].reshape(H0, K0, D), g["L0_xattn_w_kc_q"], g["L0_xattn_w_kc_kv"],
                                 g["L0_xattn_Wo"].T.reshape(H0, K0, D)], axis=2)
    n["l0x_r"] = np.concatenate([g["L0_xattn_W_qr"].transpose(0, 2, 1), g["L0_xattn_W_kr"].transpose(0, 2, 1)], axis=2)

    def chunks(a):
        return T(a.reshape(-1, P, a.shape[1]).transpose(1, 0, 2))

    n["attn_w"] = np.concatenate([chunks(g["L0_attn_" + w]) for w in ("Wq", "Wk", "Wv", "Wo")], axis=2)
    n["xattn_w"] = np.concatenate([chunks(T(g["L1_xattn_Wq"].T)), chunks(T(g["L1_xattn_Wout"].T))], axis=2)
    n["xattn_kv"] = T(g["L1_xattn_Wkv_expand"].T)
    n["ffn_ug"] = chunks(T(np.concatenate([g["L0_ffn_W_up"], g["L0_ffn_W_gate"]], axis=0).T))
    n["ffn_ws"] = g["L0_ffn_Wscale_ug"].reshape(1, -1)
    n["ffn_dn"] = chunks(T(g["L0_ffn_W_down"].T))
    n["ffn_wsd"] = g["L0_ffn_Wscale_dp"].reshape(1, -1)
    n["ffn_su"] = T(g["L0_ffn_SU_ug"].reshape(DC, P).T)
    n["ffn_sud"] = T(g["L0_ffn_SU_dp"].reshape(IC, P).T)
    wqkv = chunks(T(g["L1_attn_W_qkv"].T))
    wz = chunks(T(g["L1_attn_W_z"].T))
    cw = g["L1_attn_conv_w"].reshape(-1, P, 4)
    wo = chunks(T(g["L1_attn_W_out"].T))
    packs = []
    for j in range(HK):
        blocks = (HK + j, j, 2 * HK + 2 * j, 2 * HK + 2 * j + 1)
        packs.append(np.concatenate(
            [np.concatenate([wqkv[:, :, b * P:(b + 1) * P] for b in blocks], axis=2).reshape(P, -1),
             wz[:, :, j * 2 * DK:(j + 1) * 2 * DK].reshape(P, -1),
             wo[:, 2 * j:2 * j + 2, :].reshape(P, -1)] + [cw[b] for b in blocks], axis=1))
    n["gdn_w"] = np.stack(packs)
    n["gdn_ab"] = chunks(T(np.concatenate([g["L1_attn_W_a"], g["L1_attn_W_b"]], axis=0).T))
    n["gdn_al"], n["gdn_dt"] = g["L1_attn_A_log"].reshape(1, -1), g["L1_attn_dt_bias"].reshape(1, -1)
    n["gdn_nw"] = g["L1_attn_norm_w"].reshape(-1, 1)
    n["moe_gate"] = chunks(T(g["L1_ffn_gate_w"].T))
    n["moe_g"] = chunks(T(g["L1_ffn_Wg"].reshape(-1, D).T))
    n["moe_u"] = chunks(T(g["L1_ffn_Wu"].reshape(-1, D).T))
    n["moe_d"] = chunks(T(g["L1_ffn_Wd"].transpose(0, 2, 1).reshape(-1, D)))
    return {k: T(v) for k, v in n.items()}


PHASES = 5


def kernel(**inputs):
    import concourse.bacc as _bacc
    from concourse.bass_utils import run_bass_kernel_spmd as _run

    nc = _bacc.Bacc("TRN2", target_bir_lowering=False, num_devices=1)
    arrays, args = {}, {}
    for name, a in layouts(inputs).items():
        arrays[f"in_{name}"] = a
        args[name] = nc.dram_tensor(f"in_{name}", a.shape, mybir.dt.from_np(a.dtype), kind="ExternalInput").ap()
    out = nc.dram_tensor("out_x", (B, S, D), F32, kind="ExternalOutput").ap()
    build(nc, args, out, PHASES)
    r = _run(nc, [arrays], core_ids=[0])
    return r.results[0]["out_x"]
```

```python
import numpy as np
import concourse.bass as bass
from concourse import mybir
from contextlib import ExitStack

F32 = mybir.dt.float32
ALU = mybir.AluOpType
ACT = mybir.ActivationFunctionType
AX = mybir.AxisListType

P = 128
B, S, D = 16, 64, 256
TILES = B * S // P
DC = D // P
L, DCTX = 128, 64
H0, K0, CQ, R0 = 16, 128, 192, 64
HQ = CQ // 2
NH, HD = 16, 16
PAIRS = NH // 2
INTER = 1024
IC = INTER // P
HK, HV, DK = 16, 32, 128
NE, TOPK, EI = 32, 8, 96
MC = NE * EI // P
MB = NE * EI // 512
LEVELS = 6
BIG = 1e30


def shape_constants():
    cols, at = [], {}

    def put(name, a):
        a = np.asarray(a, np.float32)
        full = np.zeros((P, a.shape[1]), np.float32)
        full[:a.shape[0]] = a
        at[name] = (sum(c.shape[1] for c in cols), a.shape[1])
        cols.append(full)

    def rope(length, dim):
        inv = (np.float32(1.0) / np.float32(10000.0) ** (np.arange(0, dim, 2, dtype=np.float32) / np.float32(dim))).astype(np.float32)
        f = np.arange(length, dtype=np.float32)[:, None] * inv[None, :]
        return np.repeat(np.sin(f), 2, axis=-1), np.repeat(np.cos(f), 2, axis=-1)

    i, j = np.arange(P)[:, None], np.arange(P)[None, :]
    t, s = np.arange(P)[:, None] % S, np.arange(S)[None, :]
    put("ident", i == j)
    put("cumsum", (i <= j) & (i // S == j // S))
    had = np.array([[(-1.0) ** bin(a & b).count("1") for b in range(P)] for a in range(P)])
    put("had", had)
    put("nhad", -had)
    put("eye", t == s)
    put("tril", t >= s)
    put("strict", t > s)
    put("neg", np.where(t >= s, 0.0, -BIG))
    for k in range(LEVELS):
        w = 1 << k
        put(f"lvl{k}", (t // (2 * w) == s // (2 * w)) & (t // w % 2 == 1) & (s // w % 2 == 0))
    put("head", np.arange(P)[:, None] // HD == np.arange(P // HD)[None, :])
    put("mhalf", np.full((P, 32), -0.5))
    put("ones", np.ones((P, 1)))
    sq, cq = rope(S, CQ)
    put("cosq", np.concatenate([cq[:, :HQ].T, cq[:, HQ:].T], axis=1))
    put("sinq", np.concatenate([sq[:, :HQ].T, sq[:, HQ:].T], axis=1))
    sk, ck = rope(L, DCTX)
    sk = sk * np.where(np.arange(DCTX) < DCTX // 2, -1.0, 1.0)
    put("cosk", ck)
    put("sink", sk)
    put("coskT", ck.T)
    put("sinkT", sk.T)
    return np.concatenate(cols, axis=1), at


CONSTS, CONST_AT = shape_constants()


def build(nc, d, out):
    root = ExitStack()
    with root:
        def sb(ctx, name, shape):
            return ctx.enter_context(nc.sbuf_tensor(name, shape, F32))

        def semaphores(ctx, names, phase=""):
            made = {n: nc.alloc_semaphore(phase + n) for n in names.split()}

            def retire():
                nc.clear_and_free_semaphores(list(made.values()))
                nc.all_engine_barrier()

            ctx.callback(retire)
            return made

        X = sb(root, "X", [P, TILES, D])
        con = sb(root, "con", [P, CONSTS.shape[1]])
        HT = sb(root, "HT", [P, DC, B * S])
        bn = sb(root, "bn", [P, 2, 6])
        mv = sb(root, "mv", [P, 2, 2])
        ve = sb(root, "ve", [P, 2, 1])
        rstd = sb(root, "rstd", [P, 2, 1])
        hn = sb(root, "hn", [P, 2, D])
        carrier = sb(root, "carrier", [P, 1])
        PS = root.enter_context(nc.psum_tensor("PS", [P, 8, 512], F32))

        def C(name, rows=P):
            o, n = CONST_AT[name]
            return con[0:rows, o:o + n]

        def over(ap, n):
            return ap.unsqueeze(1).broadcast_to([ap.shape[0], n, ap.shape[1]])

        def each(ap, n):
            return ap.unsqueeze(2).broadcast_to([ap.shape[0], ap.shape[1], n])

        def norm_stats(v, i, p, stats, n):
            v.bn_stats(bn[:, p, :], X[:, bass.ds(i * 2 + p, 1), :]).then_inc(stats, 1)
            v.wait_ge(stats, n * 4 + 1)
            v.memset(carrier[:, :], 0.0)
            v.bn_aggr(mv[:, p, :], bn[:, p, :]).then_inc(stats, 1)
            v.wait_ge(stats, n * 4 + 2)
            v.tensor_scalar(ve[:, p, :], mv[:, p, 1:2], 1e-5, None, ALU.add).then_inc(stats, 1)

        def norm_root(g, n, p, stats, rooted):
            g.wait_ge(stats, n * 4 + 3)
            g.tensor_tensor(rstd[:, p, :], ve[:, p, :], C("mhalf")[:, 0:1], ALU.pow).then_inc(rooted, 1)

        def norm_apply(v, i, p, stats, rooted, turned, n):
            v.wait_ge(turned, n + 1)
            v.wait_ge(rooted, n + 1)
            v.tensor_scalar(hn[:, p, :], X[:, bass.ds(i * 2 + p, 1), :], mv[:, p, 0:1], rstd[:, p, :],
                            ALU.subtract, ALU.mult).then_inc(stats, 1)

        def norm_turn(pe, n, p, bank, stats, turned):
            pe.wait_ge(stats, n * 4 + 4)
            for c in range(DC):
                mm = pe.transpose(PS[:, bank, c * P:(c + 1) * P], hn[:, p, c * P:(c + 1) * P], C("ident"))
            mm.then_inc(turned, 1)

        def hT_psum(bank):
            return PS[:, bank, 0:D].rearrange("p (c n) -> p c n", c=DC)

        mid = root.enter_context(ExitStack())
        kvr = sb(mid, "kvr", [P, B, DCTX])
        kvT = sb(mid, "kvT", [DCTX, B, L])
        cxT = sb(mid, "cxT", [DCTX, B, L])
        TTd = nc.dram_tensor("queries_scratch", (DCTX, B, H0, S), F32, kind="Internal").ap()
        W2 = sb(mid, "W2", [P, H0 // 2, D])
        with ExitStack() as ctx:
            cxr = sb(ctx, "cxr", [DCTX, B, L])
            cx = sb(ctx, "cx", [P, B, DCTX])
            cr = sb(ctx, "cr", [P, B, DCTX])
            s = semaphores(ctx, "p0_in p0_x p0_kv p0_dve p0_stats0 p0_stats1 p0_root0 p0_root1 p0_turned0 p0_turned1 p0_hT0 p0_hT1")
            with nc.Block() as block:
                @block.sync
                def _(sp):
                    sp.dma_start(con[:, :], d["consts"]).then_inc(s["p0_x"], 16)
                    sp.dma_start(X[:, :, :], d["x"].rearrange("(n b) s c -> (b s) n c", b=2)).then_inc(s["p0_x"], 16)
                    sp.dma_start(cxT[:, :, :], d["ctxT"]).then_inc(s["p0_in"], 16)
                    sp.dma_start(cxr[:, :, :], d["ctxT_rolled"]).then_inc(s["p0_in"], 16)
                    sp.dma_start(cx[:, :, :], d["ctx"]).then_inc(s["p0_in"], 16)
                    sp.dma_start(cr[:, :, :], d["ctx_rolled"]).then_inc(s["p0_in"], 16)

                @block.vector
                def _(v):
                    v.wait_ge(s["p0_x"], 32)
                    with v.Fori(0, TILES // 2) as i:
                        for p in range(2):
                            norm_stats(v, i, p, s[f"p0_stats{p}"], i)
                        for p in range(2):
                            norm_apply(v, i, p, s[f"p0_stats{p}"], s[f"p0_root{p}"], s[f"p0_turned{p}"], i)
                    v.wait_ge(s["p0_in"], 64)
                    v.tensor_tensor(kvT[:, :, :], cxT[:, :, :], over(C("coskT", DCTX), B), ALU.mult).then_inc(s["p0_dve"], 1)
                    v.tensor_tensor(cxr[:, :, :], cxr[:, :, :], over(C("sinkT", DCTX), B), ALU.mult).then_inc(s["p0_dve"], 1)
                    v.tensor_tensor(kvr[:, :, :], cx[:, :, :], over(C("cosk"), B), ALU.mult).then_inc(s["p0_dve"], 1)
                    v.tensor_tensor(cr[:, :, :], cr[:, :, :], over(C("sink"), B), ALU.mult).then_inc(s["p0_dve"], 1)
                    v.wait_ge(s["p0_dve"], 2)
                    v.tensor_tensor(kvT[:, :, :], kvT[:, :, :], cxr[:, :, :], ALU.add).then_inc(s["p0_kv"], 1)
                    v.wait_ge(s["p0_dve"], 4)
                    v.tensor_tensor(kvr[:, :, :], kvr[:, :, :], cr[:, :, :], ALU.add).then_inc(s["p0_kv"], 1)

                @block.gpsimd
                def _(g):
                    g.wait_ge(s["p0_x"], 32)
                    with g.Fori(0, TILES // 2) as i:
                        for p in range(2):
                            norm_root(g, i, p, s[f"p0_stats{p}"], s[f"p0_root{p}"])

                @block.tensor
                def _(pe):
                    for p in range(2):
                        pe.sem_inc(s[f"p0_turned{p}"], 1)
                    with pe.Fori(0, TILES // 2) as i:
                        for p in range(2):
                            pe.wait_ge(s[f"p0_hT{p}"], i + 1)
                            norm_turn(pe, i, p, p, s[f"p0_stats{p}"], s[f"p0_turned{p}"])

                @block.scalar
                def _(a):
                    for p in range(2):
                        a.sem_inc(s[f"p0_hT{p}"], 1)
                    with a.Fori(0, TILES // 2) as i:
                        for p in range(2):
                            a.wait_ge(s[f"p0_turned{p}"], i + 2)
                            a.activation(HT[:, :, bass.ds(i * 2 * P + p * P, P)], hT_psum(p), ACT.Copy).then_inc(s[f"p0_hT{p}"], 1)

        weights = (aw, xw, xkv, ug, dn, wsu, wsd, su, sud) = tuple(
            sb(mid, name, shape) for name, shape in
            (("aw", [P, DC, 4 * D]), ("xw", [P, DC, 2 * D]), ("xkv", [DCTX, 2 * D]), ("ug", [P, DC, 2 * INTER]), ("dn", [P, IC, D]),
             ("wsu", [P, 2 * INTER]), ("wsd", [P, D]), ("su", [P, DC]), ("sud", [P, IC])))
        KW = D + CQ + DCTX + D
        RW = CQ + DCTX
        with ExitStack() as ctx:
            wk = sb(ctx, "wk", [P, 2, KW])
            tts = sb(ctx, "tts", [DCTX, 2, 512])
            wr = sb(ctx, "wr", [R0, 2, RW])
            cw = sb(ctx, "cw", [P, 2, DC, CQ])
            mw = sb(ctx, "mw", [HQ, 2, 2, DCTX])
            ra = sb(ctx, "ra", [HQ, 2, 512])
            rb = sb(ctx, "rb", [HQ, 2, 512])
            rc = sb(ctx, "rc", [HQ, 2, 512])
            rd = sb(ctx, "rd", [HQ, 2, 512])
            r0 = sb(ctx, "r0", [HQ, 2, 512])
            r1 = sb(ctx, "r1", [HQ, 2, 512])
            s = semaphores(ctx, "p1_w0 p1_w1 p1_c p1_mw p1_w2 p1_cs p1_ms p1_w2s p1_q0 p1_q1 p1_prod0 p1_prod1 p1_rope0 p1_rope1 p1_t0 p1_t1 p1_ts0 p1_ts1 p1_st0 p1_st1 p1_next")
            with nc.Block() as block:
                @block.sync
                def _(sp):
                    def load(h, p):
                        sp.dma_start(wk[:, p, :], d["l0x_k"][bass.ds(h, 1), :, :].rearrange("a p n -> (a p) n")).then_inc(s[f"p1_w{p}"], 16)
                        sp.dma_start(wr[:, p, :], d["l0x_r"][bass.ds(h, 1), :, :].rearrange("a p n -> (a p) n")).then_inc(s[f"p1_w{p}"], 16)
                    for p in range(2):
                        load(p, p)
                        sp.sem_inc(s[f"p1_st{p}"], 16)
                    sp.dma_start(dn[:, :, :], d["ffn_dn"]).then_inc(s["p1_next"], 16)
                    sp.dma_start(wsu[:, :], d["ffn_ws"].partition_broadcast(P)).then_inc(s["p1_next"], 16)
                    sp.dma_start(ug[:, :, :], d["ffn_ug"]).then_inc(s["p1_next"], 16)
                    sp.dma_start(wsd[:, :], d["ffn_wsd"].partition_broadcast(P)).then_inc(s["p1_next"], 16)
                    sp.dma_start(su[:, :], d["ffn_su"]).then_inc(s["p1_next"], 16)
                    sp.dma_start(sud[:, :], d["ffn_sud"]).then_inc(s["p1_next"], 16)
                    sp.dma_start(aw[:, :, :], d["attn_w"]).then_inc(s["p1_next"], 16)
                    sp.dma_start(xw[:, :, :], d["xattn_w"]).then_inc(s["p1_next"], 16)
                    sp.dma_start(xkv[:, :], d["xattn_kv"]).then_inc(s["p1_next"], 16)

                    def store(h):
                        for f in range(2):
                            sp.wait_ge(s[f"p1_ts{f}"], h + 2)
                            sp.dma_start(TTd[:, f * 8:(f + 1) * 8, bass.ds(h, 1), :].rearrange("p b a s -> p b (a s)"), tts[:, f, :].rearrange("p (b s) -> p b s", s=S)).then_inc(s[f"p1_st{f}"], 16)

                    with sp.Fori(0, H0 // 2 - 1) as i:
                        for p in range(2):
                            sp.wait_ge(s["p1_w2"], i * 2 + p + 1)
                            load(i * 2 + p + 2, p)
                            store(i * 2 + p)
                    for h in (H0 - 2, H0 - 1):
                        store(h)
                    for f in range(2):
                        sp.wait_ge(s[f"p1_st{f}"], H0 * 16 + 16)
                    sp.wait_ge(s["p1_next"], 9 * 16)

                @block.tensor
                def _(pe):
                    for f in range(2):
                        pe.sem_inc(s[f"p1_t{f}"], 1)
                    def fold(i, p):
                        pe.wait_ge(s[f"p1_w{p}"], i * 32 + 32)
                        pe.wait_ge(s["p1_w2s"], i * 2 + p + 1)
                        for c in range(DC):
                            mm = pe.matmul(PS[:, 0, c * CQ:(c + 1) * CQ], wk[:, p, c * P:(c + 1) * P],
                                           wk[:, p, D:D + CQ], start=True, stop=True)
                        mm.then_inc(s["p1_c"], 1)
                        for c in range(2):
                            mm = pe.matmul(PS[0:HQ, 1, c * DCTX:(c + 1) * DCTX], wr[:, p, c * HQ:(c + 1) * HQ],
                                           wr[:, p, CQ:RW], start=True, stop=True)
                        mm.then_inc(s["p1_mw"], 1)
                        pe.matmul(PS[64 * p:64 * p + DCTX, 1, P:P + D], wk[:, p, D + CQ:D + CQ + DCTX],
                                  wk[:, p, D + CQ + DCTX:KW], start=True, stop=True).then_inc(s["p1_w2"], 1)

                    def queries(i, p, last):
                        h = i * 2 + p
                        pe.wait_ge(s["p1_cs"], h + 1)
                        for f in range(2):
                            for c in range(2):
                                for k in range(DC):
                                    mm = pe.matmul(PS[0:HQ, 2 + 2 * f + c, :], cw[:, p, k, c * HQ:(c + 1) * HQ],
                                                   HT[:, k, f * 512:(f + 1) * 512], start=(k == 0), stop=(k == DC - 1))
                            mm.then_inc(s[f"p1_q{f}"], 1)
                        pe.wait_ge(s["p1_ms"], h + 1)
                        for f in range(2):
                            pe.wait_ge(s[f"p1_rope{f}"], h * 2 + 2)
                            pe.wait_ge(s[f"p1_ts{f}"], h + 1)
                            pe.matmul(PS[0:DCTX, 6 + f, :], mw[:, p, 0, :], r0[:, f, :], start=True, stop=False)
                            pe.matmul(PS[0:DCTX, 6 + f, :], mw[:, p, 1, :], r1[:, f, :], start=False, stop=True).then_inc(s[f"p1_t{f}"], 1)
                            if f == 0 and not last:
                                fold(i + p, 1 - p)

                    fold(0, 0)
                    with pe.Fori(0, H0 // 2 - 1) as i:
                        for p in range(2):
                            queries(i, p, False)
                    for p in range(2):
                        queries(H0 // 2 - 1, p, p == 1)

                @block.scalar
                def _(a):
                    a.sem_inc(s["p1_w2s"], 1)
                    for f in range(2):
                        a.sem_inc(s[f"p1_ts{f}"], 1)

                    def folded(i, p):
                        h = i * 2 + p
                        a.wait_ge(s["p1_c"], h + 1)
                        a.activation(cw[:, p, :, :], PS[:, 0, 0:DC * CQ].rearrange("p (c n) -> p c n", c=DC), ACT.Copy).then_inc(s["p1_cs"], 1)
                        a.wait_ge(s["p1_w2"], h + 1)
                        a.activation(mw[:, p, :, :], PS[0:HQ, 1, 0:2 * DCTX].rearrange("p (c n) -> p c n", c=2), ACT.Copy).then_inc(s["p1_ms"], 1)
                        a.activation(W2[64 * p:64 * p + DCTX, bass.ds(i, 1), :], PS[64 * p:64 * p + DCTX, 1, P:P + D].unsqueeze(1), ACT.Copy).then_inc(s["p1_w2s"], 1)

                    def queries(i, p, last):
                        h = i * 2 + p
                        for f in range(2):
                            a.wait_ge(s[f"p1_t{f}"], h + 2)
                            a.wait_ge(s[f"p1_st{f}"], h * 16 + 16)
                            a.activation(tts[:, f, :], PS[0:DCTX, 6 + f, :], ACT.Copy).then_inc(s[f"p1_ts{f}"], 1)
                            if f == 0 and not last:
                                folded(i + p, 1 - p)

                    folded(0, 0)
                    with a.Fori(0, H0 // 2 - 1) as i:
                        for p in range(2):
                            queries(i, p, False)
                    for p in range(2):
                        queries(H0 // 2 - 1, p, p == 1)

                @block.vector
                def _(v):
                    def table(name, c):
                        return over(C(name, HQ)[:, c * S:(c + 1) * S], 512 // S)

                    def view(ap):
                        return ap.rearrange("p (b s) -> p b s", s=S)

                    with v.Fori(0, H0 // 2) as i:
                        for p in range(2):
                            h = i * 2 + p
                            for f in range(2):
                                prod, rope = s[f"p1_prod{f}"], s[f"p1_rope{f}"]
                                q0, q1 = view(PS[0:HQ, 2 + 2 * f, :]), view(PS[0:HQ, 3 + 2 * f, :])
                                v.wait_ge(s[f"p1_q{f}"], h + 1)
                                v.wait_ge(s[f"p1_t{f}"], h + 1)
                                v.tensor_tensor(view(ra[:, f, :]), q0, table("cosq", 0), ALU.mult).then_inc(prod, 1)
                                v.tensor_tensor(view(rb[:, f, :]), q1, table("sinq", 0), ALU.mult).then_inc(prod, 1)
                                v.tensor_tensor(view(rc[:, f, :]), q1, table("cosq", 1), ALU.mult).then_inc(prod, 1)
                                v.tensor_tensor(view(rd[:, f, :]), q0, table("sinq", 1), ALU.mult).then_inc(prod, 1)
                                v.wait_ge(prod, h * 4 + 2)
                                v.tensor_tensor(r0[:, f, :], ra[:, f, :], rb[:, f, :], ALU.subtract).then_inc(rope, 1)
                                v.wait_ge(prod, h * 4 + 4)
                                v.tensor_tensor(r1[:, f, :], rc[:, f, :], rd[:, f, :], ALU.add).then_inc(rope, 1)

        phase2(nc, d, sb, semaphores, C, over, each, X, HT, PS, carrier, bn, mv, ve, rstd, hn, kvr, kvT, cxT, TTd, W2, weights,
               norm_stats, norm_root, norm_apply, norm_turn, hT_psum)
        mid.close()
        phase3(nc, d, sb, semaphores, C, over, each, X, HT, PS, carrier)
        phase4(nc, d, sb, semaphores, C, over, each, X, PS, carrier, norm_stats, norm_root, norm_apply, norm_turn, hT_psum)

        with ExitStack() as ctx:
            s = semaphores(ctx, "stored")
            with nc.Block() as block:
                @block.sync
                def _(sp):
                    sp.dma_start(out.rearrange("(n b) s c -> (b s) n c", b=2), X[:, :, :]).then_inc(s["stored"], 16)
                    sp.wait_ge(s["stored"], 16)


def phase2(nc, d, sb, semaphores, C, over, each, X, HT, PS, carrier, bn, mv, ve, rstd, hn, kvr, kvT, cxT, TTd, W2, weights,
           norm_stats, norm_root, norm_apply, norm_turn, hT_psum):
    PER_P = ("tt sc sm ex nr tp pt cx ct out res "
             "qkv q vv kb asc asm aex anr atp apt av ot aout ares "
             "stats root turned hT "
             "fx fh fhs ug th fy fo fres")
    with ExitStack() as ctx:
        aw, xw, xkv, ug, dn, wsu, wsd, su, sud = weights
        kt = sb(ctx, "kt", [DCTX, 2, 2, L])
        kr = sb(ctx, "kr", [P, 2, 2, DCTX])
        ct = sb(ctx, "ct", [DCTX, 2, 2, S])
        ctd = sb(ctx, "ctd", [DCTX, 2, 2, 2, S])
        hTd = sb(ctx, "hTd", [P, 2, DC, 2, 2, S])
        b1 = sb(ctx, "b1", [P, 2, 2048])
        b2 = sb(ctx, "b2", [P, 2, 2048])
        b3 = sb(ctx, "b3", [P, 2, 2048])
        hT = sb(ctx, "hT", [P, 2, DC, P])
        qT = sb(ctx, "qT", [P, 2, DC, P])
        oT = sb(ctx, "oT", [P, 2, DC, P])
        vb = sb(ctx, "vb", [P, 2, 2 * PAIRS, 2, HD])
        mx = sb(ctx, "mx", [P, 2, 16])
        rs = sb(ctx, "rs", [P, 2, 16])
        s = semaphores(ctx, "f_prep f_scale f_pe f_act vzero "
                       + " ".join(f"{n}{p}" for n in PER_P.split() for p in range(2)), "p2_")
        TURNS = TILES // 2

        def tile(i, p):
            return bass.ds(i * 2 + p, 1)

        def queries(p):
            return b1[0:DCTX, p, :].rearrange("p (b g n) -> p b g n", b=2, n=P)

        def probs0(p):
            return b2[:, p, :].rearrange("p (g l) -> p g l", l=L)

        def probsT0(p, b):
            return b1[:, p, b * 1024:(b + 1) * 1024].rearrange("p (g h s) -> p g h s", h=2, s=S)

        def ctxT(p):
            return b3[:, p, 0:1024].rearrange("p (g n) -> p g n", n=P)

        def keys(p, c, b):
            o = (c * 2 + b) * 512
            return b1[:, p, o:o + 512]

        def probs(p):
            return b2[:, p, 0:1024].rearrange("p (h s) -> p h s", s=S)

        def probsT(p):
            return b3[:, p, 0:1024].rearrange("p (g n) -> p g n", n=P)

        def banks(p, a, n):
            return PS[:, 4 * p + a:4 * p + a + n, :].rearrange("p k n -> p (k n)")

        with nc.Block() as block:
            @block.sync
            def _(sp):
                def load(t, p):
                    sp.dma_start(b1[0:DCTX, p, :], TTd[:, bass.ds(t * 2, 2), :, :].rearrange("p b h s -> p (b h s)")).then_inc(s[f"tt{p}"], 16)
                    sp.dma_start(kt[:, p, :, :], kvT[:, bass.ds(t * 2, 2), :]).then_inc(s[f"tt{p}"], 16)
                    sp.dma_start(kr[:, p, :, :], kvr[:, bass.ds(t * 2, 2), :]).then_inc(s[f"tt{p}"], 16)
                    sp.dma_start(ct[:, p, :, :], cxT[:, bass.ds(t * 2, 2), 0:S]).then_inc(s[f"tt{p}"], 16)
                    for w in range(2):
                        sp.dma_start(ctd[:, p, :, w, :], cxT[:, bass.ds(t * 2, 2), 0:S]).then_inc(s[f"tt{p}"], 16)

                for p in range(2):
                    load(p, p)
                with sp.Fori(0, TURNS - 1) as i:
                    for p in range(2):
                        sp.wait_ge(s[f"aout{p}"], i * 2 + 2)
                        load(i * 2 + p + 2, p)

            @block.tensor
            def _(pe):
                for k in range(4):
                    mm = pe.matmul(PS[:, k, :], C("had"), dn[:, 2 * k:2 * k + 2, :], start=True, stop=True)
                mm.then_inc(s["f_pe"], 1)
                pe.wait_ge(s["f_act"], 1)
                pe.wait_ge(s["vzero"], 1)
                for p in range(2):
                    pe.sem_inc(s[f"turned{p}"], 1)

                def turn(i, q, p):
                    norm_turn(pe, i * 4 + q, p, 4 * p, s[f"stats{p}"], s[f"turned{p}"])

                def attention(i, a, p):
                    n = i * 2 + a
                    wq, wo = (aw[:, :, 0:D], aw[:, :, 3 * D:4 * D]) if a == 0 else (xw[:, :, 0:D], xw[:, :, D:2 * D])
                    q0, k0 = PS[:, 4 * p + 2, 0:D], PS[:, 4 * p, D:2 * D]
                    pe.wait_ge(s[f"hT{p}"], i * 3 + a + 2)
                    for c in range(DC):
                        for k in range(DC):
                            pe.matmul(q0[:, c * P:(c + 1) * P], wq[:, k, c * P:(c + 1) * P], hT[:, p, k, :],
                                      start=(k == 0), stop=(k == DC - 1))
                    for c in range(DC):
                        if a == 0:
                            for k in range(DC):
                                pe.matmul(k0[:, c * P:(c + 1) * P], aw[:, k, D + c * P:D + (c + 1) * P], hT[:, p, k, :],
                                          start=(k == 0), stop=(k == DC - 1))
                        else:
                            pe.matmul(k0[:, c * P:(c + 1) * P], xkv[:, c * P:(c + 1) * P], ct[:, p, :, :],
                                      start=True, stop=True)
                    for b in range(2):
                        if a == 0:
                            for k in range(DC):
                                mm = pe.matmul(PS[:, 4 * p + 1, b * D:(b + 1) * D], hTd[:, p, k, b, :, :].rearrange("p w s -> p (w s)"),
                                               aw[:, k, 2 * D:3 * D], start=(k == 0), stop=(k == DC - 1))
                        else:
                            mm = pe.matmul(PS[:, 4 * p + 1, b * D:(b + 1) * D], ctd[:, p, b, :, :].rearrange("p w s -> p (w s)"),
                                           xkv[:, D:2 * D], start=True, stop=True)
                    mm.then_inc(s[f"qkv{p}"], 1)

                def scores(i, a, p):
                    n = i * 2 + a
                    pe.wait_ge(s[f"q{p}"], n + 1)
                    pe.wait_ge(s[f"kb{p}"], n * 4 + 4)
                    for c in range(DC):
                        for b in range(2):
                            mm = pe.matmul(PS[64 * b:64 * b + S, 4 * p + 2 + c, :], qT[:, p, c, b * S:(b + 1) * S],
                                           keys(p, c, b), start=True, stop=True)
                    mm.then_inc(s[f"asc{p}"], 1)

                def probs_turn(i, a, p):
                    n = i * 2 + a
                    pe.wait_ge(s[f"anr{p}"], n * 3 + 3)
                    pe.wait_ge(s[f"vv{p}"], n * 2 + 2)
                    for g in range(PAIRS):
                        mm = pe.transpose(PS[:, 4 * p + g // 4, (g % 4) * P:(g % 4 + 1) * P],
                                          b2[:, p, g * P:(g + 1) * P], C("ident"))
                    mm.then_inc(s[f"atp{p}"], 1)

                def values(i, a, p):
                    n = i * 2 + a
                    pe.wait_ge(s[f"apt{p}"], n + 1)
                    for b in range(2):
                        for g in range(PAIRS):
                            r = 32 * (g % 4)
                            o = (g // 4) * P + b * S
                            mm = pe.matmul(PS[r:r + 32, 4 * p + 2, o:o + S],
                                           vb[:, p, b * PAIRS + g, :, :].rearrange("p h d -> p (h d)"),
                                           probsT(p)[:, g, b * S:(b + 1) * S], start=True, stop=True,
                                           tile_position=(0, r))
                    mm.then_inc(s[f"av{p}"], 1)

                def project(i, a, p):
                    n = i * 2 + a
                    wo = aw[:, :, 3 * D:4 * D] if a == 0 else xw[:, :, D:2 * D]
                    pe.wait_ge(s[f"ot{p}"], n + 1)
                    for k in range(DC):
                        mm = pe.matmul(PS[:, 4 * p + 3, 0:D], oT[:, p, k, :], wo[:, k, :], start=(k == 0), stop=(k == DC - 1))
                    mm.then_inc(s[f"aout{p}"], 1)

                def narrow(i, a):
                    for step in (attention, scores, probs_turn, values, project):
                        for p in range(2):
                            step(i, a, p)

                with pe.Fori(0, TURNS) as i:
                    for p in range(2):
                        pe.wait_ge(s[f"tt{p}"], i * 96 + 96)
                        pe.wait_ge(s[f"hT{p}"], i * 3 + 1)
                        for b in range(2):
                            for g in range(H0 // 2):
                                mm = pe.matmul(PS[:, 4 * p + 2 * b + g // 4, (g % 4) * L:(g % 4 + 1) * L],
                                               queries(p)[:, b, g, :],
                                               kt[:, p, b, :], start=True, stop=True)
                            mm.then_inc(s[f"sc{p}"], 1)
                    for p in range(2):
                        pe.wait_ge(s[f"nr{p}"], i * 3 + 3)
                        for b in range(2):
                            for g in range(H0 // 2):
                                mm = pe.transpose(PS[:, 4 * p + 2 * b + g // 4, (g % 4) * P:(g % 4 + 1) * P],
                                                  probs0(p)[:, b * 8 + g, :], C("ident"))
                            mm.then_inc(s[f"tp{p}"], 1)
                    for p in range(2):
                        for b in range(2):
                            pe.wait_ge(s[f"pt{p}"], i * 2 + b + 1)
                            for h in range(2):
                                mm = pe.matmul(PS[64 * h:64 * h + DCTX, 4 * p + 2 * b, :], kr[:, p, b, :],
                                               probsT0(p, b)[:, :, h, :], start=True, stop=True)
                            mm.then_inc(s[f"cx{p}"], 1)
                    for p in range(2):
                        pe.wait_ge(s[f"ct{p}"], i * 2 + 2)
                        for g in range(H0 // 2):
                            mm = pe.matmul(PS[:, 4 * p + 1, 0:D], ctxT(p)[:, g, :], W2[:, g, :],
                                           start=(g == 0), stop=(g == H0 // 2 - 1))
                        mm.then_inc(s[f"out{p}"], 1)
                    for p in range(2):
                        turn(i, 0, p)
                    narrow(i, 0)
                    for p in range(2):
                        turn(i, 1, p)
                    for p in range(2):
                        pe.wait_ge(s[f"fx{p}"], i + 1)
                        for c in range(DC):
                            pe.matmul(PS[:, 4 * p + 1, c * P:(c + 1) * P], C("had"), hT[:, p, 0, :], start=True, stop=False)
                            mm = pe.matmul(PS[:, 4 * p + 1, c * P:(c + 1) * P], C("nhad" if c else "had"), hT[:, p, 1, :],
                                           start=False, stop=True)
                        mm.then_inc(s[f"fh{p}"], 1)
                    pe.wait_ge(s["f_scale"], 2)
                    for p in range(2):
                        pe.wait_ge(s[f"fhs{p}"], i + 1)
                        for m in range(2 * IC):
                            for k in range(DC):
                                mm = pe.matmul(PS[:, 4 * p + m // 4, (m % 4) * P:(m % 4 + 1) * P], ug[:, k, m * P:(m + 1) * P],
                                               qT[:, p, k, :], start=(k == 0), stop=(k == DC - 1))
                        mm.then_inc(s[f"ug{p}"], 1)
                    for p in range(2):
                        pe.wait_ge(s[f"fy{p}"], i * 2 + 2)
                        for m in range(IC):
                            mm = pe.matmul(PS[:, 4 * p, 0:D], b3[:, p, m * P:(m + 1) * P], dn[:, m, :],
                                           start=(m == 0), stop=(m == IC - 1))
                        mm.then_inc(s[f"fo{p}"], 1)
                    for p in range(2):
                        turn(i, 2, p)
                    narrow(i, 1)
                    for p in range(2):
                        turn(i, 3, p)

            @block.scalar
            def _(a):
                a.wait_ge(s["f_pe"], 1)
                a.activation(b2[:, 0, :], PS[:, 0:4, :].rearrange("p k n -> p (k n)"), ACT.Copy).then_inc(s["f_act"], 1)
                for p in range(2):
                    a.sem_inc(s[f"hT{p}"], 1)

                def copy_hT(i, q, p):
                    n = i * 4 + q
                    a.wait_ge(s[f"turned{p}"], n + 2)
                    if q == 1:
                        for c in range(DC):
                            x = a.activation(hT[:, p, c, :], PS[:, 4 * p, c * P:(c + 1) * P], ACT.Copy, scale=su[:, c:c + 1])
                        x.then_inc(s[f"fx{p}"], 1)
                    elif q == 3:
                        a.activation(HT[:, :, bass.ds(i * 2 * P + p * P, P)], hT_psum(4 * p), ACT.Copy).then_inc(s[f"hT{p}"], 1)
                    else:
                        if q == 0:
                            for w in range(2):
                                a.activation(hTd[:, p, :, :, w, :].rearrange("p c b s -> p (c b) s"),
                                             PS[:, 4 * p, 0:D].rearrange("p (g s) -> p g s", s=S), ACT.Copy)
                        a.activation(hT[:, p, :, :], hT_psum(4 * p), ACT.Copy).then_inc(s[f"hT{p}"], 1)

                def narrow(i, k):
                    n = i * 2 + k
                    for p in range(2):
                        a.wait_ge(s[f"qkv{p}"], n + 1)
                        a.activation(qT[:, p, :, :], PS[:, 4 * p + 2, 0:D].rearrange("p (c n) -> p c n", c=DC), ACT.Copy).then_inc(s[f"q{p}"], 1)
                        for h in range(2):
                            r = slice(64 * h, 64 * h + S)
                            a.activation(vb[r, p, :, h, :], PS[r, 4 * p + 1, :].rearrange("p (g h d) -> p g h d", h=2, d=HD)[:, :, h, :],
                                         ACT.Copy).then_inc(s[f"vv{p}"], 1)
                    for p in range(2):
                        a.wait_ge(s[f"asm{p}"], n * 3 + 3)
                        a.activation(probs(p), probs(p), ACT.Exp, scale=(1.0 / 8, 1.0 / 4)[k]).then_inc(s[f"aex{p}"], 1)
                    for p in range(2):
                        a.wait_ge(s[f"atp{p}"], n + 1)
                        a.activation(b3[:, p, 0:1024], banks(p, 0, 2), ACT.Copy).then_inc(s[f"apt{p}"], 1)
                    for p in range(2):
                        a.wait_ge(s[f"av{p}"], n + 1)
                        a.activation(oT[:, p, :, :], PS[:, 4 * p + 2, 0:D].rearrange("p (c n) -> p c n", c=DC), ACT.Copy).then_inc(s[f"ot{p}"], 1)

                with a.Fori(0, TURNS) as i:
                    for p in range(2):
                        for b in range(2):
                            a.wait_ge(s[f"sm{p}"], i * 4 + 2 * b + 2)
                            x = probs0(p)[:, b * 8:(b + 1) * 8, :]
                            a.activation(x, x, ACT.Exp).then_inc(s[f"ex{p}"], 1)
                    for p in range(2):
                        for b in range(2):
                            a.wait_ge(s[f"tp{p}"], i * 2 + b + 1)
                            a.activation(b1[:, p, b * 1024:(b + 1) * 1024], banks(p, 2 * b, 2), ACT.Copy).then_inc(s[f"pt{p}"], 1)
                    for p in range(2):
                        for b in range(2):
                            a.wait_ge(s[f"cx{p}"], i * 2 + b + 1)
                            a.activation(ctxT(p)[:, :, b * S:(b + 1) * S], PS[:, 4 * p + 2 * b, :].rearrange("p (g s) -> p g s", s=S),
                                         ACT.Copy).then_inc(s[f"ct{p}"], 1)
                    for p in range(2):
                        copy_hT(i, 0, p)
                    narrow(i, 0)
                    for p in range(2):
                        copy_hT(i, 1, p)
                    for p in range(2):
                        a.wait_ge(s[f"fh{p}"], i + 1)
                        a.activation(qT[:, p, :, :], PS[:, 4 * p + 1, 0:D].rearrange("p (c n) -> p c n", c=DC), ACT.Copy,
                                     scale=D ** -0.5).then_inc(s[f"fhs{p}"], 1)
                    for p in range(2):
                        a.wait_ge(s[f"ug{p}"], i + 1)
                        a.activation(b2[:, p, 0:1024], banks(p, 2, 2), ACT.Tanh, scale=0.5).then_inc(s[f"th{p}"], 1)
                    for p in range(2):
                        copy_hT(i, 2, p)
                    narrow(i, 1)
                    for p in range(2):
                        copy_hT(i, 3, p)

            @block.gpsimd
            def _(g):
                g.memset(vb[:, :, :, :, :], 0.0).then_inc(s["vzero"], 1)
                for k in range(DC):
                    g.tensor_tensor(ug[:, k, :], ug[:, k, :], wsu[:, :], ALU.mult)
                g.wait_ge(s["f_prep"], 7)
                g.tensor_tensor(dn[:, :, :], dn[:, :, :], each(sud[:, :], D), ALU.mult).then_inc(s["f_scale"], 1)
                g.wait_ge(s["f_scale"], 1)
                g.tensor_tensor(dn[:, :, :], dn[:, :, :], over(wsd[:, :], IC), ALU.mult).then_inc(s["f_scale"], 1)
                with g.Fori(0, TURNS) as i:
                    for q in range(4):
                        for p in range(2):
                            norm_root(g, i * 4 + q, p, s[f"stats{p}"], s[f"root{p}"])

            @block.vector
            def _(v):
                prep = s["f_prep"]
                v.wait_ge(s["f_act"], 1)
                src, k = b2[:, 0, :], 0
                for st, dst in ((1, b3[:, 0, :]), (2, b2[:, 1, :]), (4, dn[:, :, :].rearrange("p c n -> p (c n)"))):
                    a0 = src.rearrange("p (g two n) -> p g two n", two=2, n=st * D)
                    o0 = dst.rearrange("p (g two n) -> p g two n", two=2, n=st * D)
                    if k:
                        v.wait_ge(prep, k)
                    v.tensor_tensor(o0[:, :, 0, :], a0[:, :, 0, :], a0[:, :, 1, :], ALU.add).then_inc(prep, 1)
                    v.tensor_tensor(o0[:, :, 1, :], a0[:, :, 0, :], a0[:, :, 1, :], ALU.subtract).then_inc(prep, 1)
                    src, k = dst, k + 2
                v.tensor_scalar(sud[:, :], sud[:, :], INTER ** -0.5 / 2, None, ALU.mult).then_inc(prep, 1)

                def softmax_tail(x, p, sem, n):
                    v.tensor_reduce(rs[:, p, :], x, AX.X, ALU.add).then_inc(sem, 1)
                    v.wait_ge(sem, n * 3 + 1)
                    v.reciprocal(rs[:, p, :], rs[:, p, :]).then_inc(sem, 1)
                    v.wait_ge(sem, n * 3 + 2)
                    v.tensor_tensor(x, x, each(rs[:, p, :], x.shape[2]), ALU.mult).then_inc(sem, 1)

                def residual(i, p, bank, ready, n, done):
                    v.wait_ge(ready, n)
                    v.tensor_tensor(X[:, tile(i, p), :], X[:, tile(i, p), :], PS[:, bank, 0:D].unsqueeze(1), ALU.add).then_inc(done, 1)

                def norm(i, q, done, n):
                    for p in range(2):
                        v.wait_ge(s[f"{done}{p}"], n)
                        v.memset(carrier[:, :], 0.0)
                        norm_stats(v, i, p, s[f"stats{p}"], i * 4 + q)
                    for p in range(2):
                        norm_apply(v, i, p, s[f"stats{p}"], s[f"root{p}"], s[f"turned{p}"], i * 4 + q)

                def narrow(i, a):
                    n = i * 2 + a
                    for p in range(2):
                        v.wait_ge(s[f"qkv{p}"], n + 1)
                        for c in range(DC):
                            for b in range(2):
                                o = D + c * P + b * S
                                v.tensor_tensor(keys(p, c, b).rearrange("p (h s) -> p h s", s=S),
                                                over(PS[:, 4 * p, o:o + S], 8), each(C("head"), S), ALU.mult).then_inc(s[f"kb{p}"], 1)
                    for p in range(2):
                        x = probs(p)
                        sem = s[f"asm{p}"]
                        v.wait_ge(s[f"asc{p}"], n + 1)
                        v.tensor_tensor(x, banks(p, 2, 2).rearrange("p (h s) -> p h s", s=S), over(C("tril" if a == 0 else "neg"), NH),
                                        ALU.mult if a == 0 else ALU.add).then_inc(sem, 1)
                        v.wait_ge(sem, n * 3 + 1)
                        v.tensor_reduce(mx[:, p, :], x, AX.X, ALU.max).then_inc(sem, 1)
                        v.wait_ge(sem, n * 3 + 2)
                        v.tensor_tensor(x, x, each(mx[:, p, :], S), ALU.subtract).then_inc(sem, 1)
                    for p in range(2):
                        v.wait_ge(s[f"aex{p}"], n + 1)
                        softmax_tail(probs(p), p, s[f"anr{p}"], n)
                    for p in range(2):
                        residual(i, p, 4 * p + 3, s[f"aout{p}"], n + 1, s[f"ares{p}"])

                with v.Fori(0, TURNS) as i:
                    for p in range(2):
                        for b in range(2):
                            g = slice(b * 8, (b + 1) * 8)
                            x, sem = banks(p, 2 * b, 2).rearrange("p (g l) -> p g l", l=L), s[f"sm{p}"]
                            v.wait_ge(s[f"sc{p}"], i * 2 + b + 1)
                            v.tensor_reduce(mx[:, p, g], x, AX.X, ALU.max).then_inc(sem, 1)
                            v.wait_ge(sem, i * 4 + 2 * b + 1)
                            v.tensor_tensor(probs0(p)[:, g, :], x, each(mx[:, p, g], L), ALU.subtract).then_inc(sem, 1)
                    for p in range(2):
                        v.wait_ge(s[f"ex{p}"], i * 2 + 2)
                        softmax_tail(probs0(p), p, s[f"nr{p}"], i)
                    for p in range(2):
                        residual(i, p, 4 * p + 1, s[f"out{p}"], i + 1, s[f"res{p}"])
                    norm(i, 0, "res", i + 1)
                    narrow(i, 0)
                    norm(i, 1, "ares", i * 2 + 1)
                    for p in range(2):
                        v.wait_ge(s[f"th{p}"], i + 1)
                        v.scalar_tensor_tensor(b3[:, p, 0:1024], b2[:, p, 0:1024], 1.0, banks(p, 2, 2), ALU.add, ALU.mult).then_inc(s[f"fy{p}"], 1)
                        v.wait_ge(s[f"fy{p}"], i * 2 + 1)
                        v.tensor_tensor(b3[:, p, 0:1024], b3[:, p, 0:1024], banks(p, 0, 2), ALU.mult).then_inc(s[f"fy{p}"], 1)
                    for p in range(2):
                        residual(i, p, 4 * p, s[f"fo{p}"], i + 1, s[f"fres{p}"])
                    norm(i, 2, "fres", i + 1)
                    narrow(i, 1)
                    norm(i, 3, "ares", i * 2 + 2)


def phase3(nc, d, sb, semaphores, C, over, each, X, HT, PS, carrier):
    TK = B * S
    with ExitStack() as ctx:
        ga = sb(ctx, "ga", [P, TILES, 2 * HV])
        with ExitStack() as c2:
            wab = sb(c2, "wab", [P, DC, 2 * HV])
            al = sb(c2, "al", [P, HV])
            dtb = sb(c2, "dtb", [P, HV])
            ab = sb(c2, "ab", [P, TILES, 2 * HV])
            e = sb(c2, "e", [P, TILES, 2 * HV])
            s = semaphores(c2, "ab_in ab_mm ab_v ab_a")
            av, bv = ab[:, :, 0:HV], ab[:, :, HV:2 * HV]
            ea, eb = e[:, :, 0:HV], e[:, :, HV:2 * HV]
            with nc.Block() as block:
                @block.sync
                def _(sp):
                    sp.dma_start(wab[:, :, :], d["gdn_ab"]).then_inc(s["ab_in"], 16)
                    sp.dma_start(al[:, :], d["gdn_al"].partition_broadcast(P)).then_inc(s["ab_in"], 16)
                    sp.dma_start(dtb[:, :], d["gdn_dt"].partition_broadcast(P)).then_inc(s["ab_in"], 16)

                @block.tensor
                def _(pe):
                    pe.wait_ge(s["ab_in"], 48)
                    for n in range(TILES):
                        for k in range(DC):
                            mm = pe.matmul(PS[:, 0, n * 2 * HV:(n + 1) * 2 * HV], HT[:, k, n * P:(n + 1) * P], wab[:, k, :],
                                           start=(k == 0), stop=(k == DC - 1))
                    mm.then_inc(s["ab_mm"], 1)

                @block.vector
                def _(v):
                    ps = PS[:, 0, :].rearrange("p (n h) -> p n h", n=TILES)
                    v.wait_ge(s["ab_mm"], 1)
                    v.tensor_tensor(av, ps[:, :, 0:HV], over(dtb[:, :], TILES), ALU.add).then_inc(s["ab_v"], 1)
                    v.tensor_scalar(bv, ps[:, :, HV:2 * HV], -1.0, 80.0, ALU.mult, ALU.min).then_inc(s["ab_v"], 1)
                    v.wait_ge(s["ab_a"], 1)
                    v.tensor_scalar(eb, eb, 1.0, None, ALU.add).then_inc(s["ab_v"], 1)
                    v.wait_ge(s["ab_v"], 3)
                    v.reciprocal(ga[:, :, HV:2 * HV], eb)
                    v.wait_ge(s["ab_a"], 5)
                    v.tensor_scalar(av, av, 0.0, None, ALU.max).then_inc(s["ab_v"], 1)
                    v.wait_ge(s["ab_v"], 4)
                    v.tensor_tensor(av, av, ea, ALU.add).then_inc(s["ab_v"], 1)
                    v.tensor_scalar(al[:, :], al[:, :], -1.0, None, ALU.mult).then_inc(s["ab_v"], 1)
                    v.wait_ge(s["ab_v"], 6)
                    v.tensor_tensor(ga[:, :, 0:HV], av, over(al[:, :], TILES), ALU.mult)

                @block.scalar
                def _(a):
                    a.wait_ge(s["ab_v"], 2)
                    a.activation(eb, bv, ACT.Exp).then_inc(s["ab_a"], 1)
                    a.activation(al[:, :], al[:, :], ACT.Exp).then_inc(s["ab_a"], 1)
                    a.activation(ea, av, ACT.Abs).then_inc(s["ab_a"], 1)
                    a.wait_ge(s["ab_a"], 3)
                    a.activation(ea, ea, ACT.Exp, scale=-1.0).then_inc(s["ab_a"], 1)
                    a.wait_ge(s["ab_a"], 4)
                    a.activation(ea, ea, ACT.Ln, bias=1.0).then_inc(s["ab_a"], 1)

        NW = DC * 4 * DK
        ZW = DC * 2 * DK
        wp = sb(ctx, "wp", [P, NW])
        wz = sb(ctx, "wz", [P, ZW])
        wc = sb(ctx, "wc", [P, 16])
        wo = sb(ctx, "wo", [P, 2, D])
        nw = sb(ctx, "nw", [P, 1])
        gj = sb(ctx, "gj", [P, TILES, 4])
        gm = sb(ctx, "gm", [P, 2, TILES, S])
        E = sb(ctx, "E", [P, 2, TILES, S])
        Et = sb(ctx, "Et", [P, 2, TILES, S])
        acc = sb(ctx, "acc", [P, 2, 512])
        th = sb(ctx, "th", [P, 2, 512])
        y = sb(ctx, "y", [P, 4, TK])
        sq = sb(ctx, "sq", [P, 2, TK])
        z2 = sb(ctx, "z2", [P, TILES, 2, DK])
        nm = sb(ctx, "nm", [P, 2 * TILES])
        rr = sb(ctx, "rr", [P, 2 * TILES])
        rq = sb(ctx, "rq", [P, 2, TILES])
        bk = sb(ctx, "bk", [P, 2, TILES])
        dd = sb(ctx, "dd", [P, 2, TILES])
        A = sb(ctx, "A", [P, 2, TILES, 2, S])
        Pd = sb(ctx, "Pd", [P, 2, TILES, 2, S])
        AT = sb(ctx, "AT", [P, 2, TILES, P])
        T = sb(ctx, "T", [P, 2, TILES, 2, S])
        TT = sb(ctx, "TT", [P, 2, TILES, P])
        PT = sb(ctx, "PT", [P, 2, TILES, P])
        Xs = sb(ctx, "Xs", [P, 2, TILES, S])
        V = sb(ctx, "V", [P, 2, TILES, DK])
        dl = sb(ctx, "dl", [P, 2, TILES, DK])
        ms = sb(ctx, "ms", [P, 2, TILES])
        s = semaphores(ctx, "win zin cin oin nin zz zt z2 pj tap conv th y sq ss kk gj gm dps e et ed nm rr rq av pd vt vc vs at ats "
                            "pt pts ti tt tts x xs yy tu dl ds u us ms fz og0 og1 gz ogt ogs wo xa wof zero", "p3_")
        NQ = 8
        TOP = LEVELS - 1

        def wide(b0):
            return PS[:, b0:b0 + 2, :].rearrange("p k n -> p (k n)")

        def own(hv):
            return 6 if hv == 0 else 2

        def slot(h, q):
            return 0 if q < 4 and not isinstance(h, int) else q % 2

        def twice(ap):
            return ap.unsqueeze(2).broadcast_to([P, TILES, 2, S])

        def blocks(ap, b):
            return ap[64 * b:64 * b + S, :, 64 * b:64 * b + S]

        def bank(k):
            return PS[:, k, :].rearrange("p (n s) -> p n s", s=S)

        def flat(ap):
            return ap.rearrange("p n c -> p (n c)")

        LAST = HK - 1
        with nc.Block() as block:
            @block.sync
            def _(sp):
                def head(j):
                    return d["gdn_w"][bass.ds(j, 1), :, :].rearrange("a p n -> (a p) n")

                def load_kqv(j):
                    sp.dma_start(wp[:, :], head(j)[:, 0:NW]).then_inc(s["win"], 16)

                def load_taps(j):
                    sp.dma_start(wc[:, :], head(j)[:, NW + ZW + 2 * D:]).then_inc(s["cin"], 16)

                def load_z(j):
                    sp.dma_start(wz[:, :], head(j)[:, NW:NW + ZW]).then_inc(s["zin"], 16)

                def load_out(j):
                    sp.dma_start(wo[:, :, :].rearrange("p c n -> p (c n)"), head(j)[:, NW + ZW:NW + ZW + 2 * D]).then_inc(s["oin"], 16)

                def next_out(j):
                    sp.wait_ge(s["zz"], j * 4 + 4)
                    load_z(j + 1)
                    sp.wait_ge(s["wo"], j * 2 + 2)
                    load_out(j + 1)

                load_kqv(0)
                load_taps(0)
                load_z(0)
                load_out(0)
                sp.dma_start(nw[:, :], d["gdn_nw"]).then_inc(s["nin"], 16)
                sp.wait_ge(s["pj"], NQ)
                load_kqv(1)
                sp.wait_ge(s["conv"], NQ * 3)
                load_taps(1)
                with sp.Fori(0, LAST - 1) as j:
                    sp.wait_ge(s["zz"], j * 4 + 4)
                    load_z(j + 1)
                    sp.wait_ge(s["pj"], j * NQ + 2 * NQ)
                    load_kqv(j + 2)
                    sp.wait_ge(s["conv"], j * 24 + 48)
                    load_taps(j + 2)
                    sp.wait_ge(s["wo"], j * 2 + 2)
                    load_out(j + 1)
                next_out(LAST - 1)

            @block.tensor
            def _(pe):
                def project(h, q):
                    c, f = q // 2, q % 2
                    if q == 0:
                        pe.wait_ge(s["win"], h * 16 + 16)
                    if isinstance(h, int):
                        if q >= 2:
                            pe.wait_ge(s["conv"], (q - 1) * 3)
                    elif q == 0:
                        pe.wait_ge(s["vc"], h * 2)
                    elif q <= 4:
                        pe.wait_ge(s["conv"], h * 24 + q * 3)
                    elif q == 5:
                        pe.wait_ge(s["z2"], h * 4)
                    else:
                        pe.wait_ge(s["conv"], h * 24 + (q - 1) * 3)
                    for k in range(DC):
                        o = k * 4 * DK + c * DK
                        mm = pe.matmul(PS[:, slot(h, q), :], wp[:, o:o + DK], HT[:, k, f * 512:(f + 1) * 512],
                                       start=(k == 0), stop=(k == DC - 1))
                    mm.then_inc(s["pj"], 1)

                def project_z(j, m):
                    if m == 0:
                        pe.wait_ge(s["zin"], j * 16 + 16)
                        pe.wait_ge(s["vc"], j * 2 + 2)
                    else:
                        pe.wait_ge(s["z2"], j * 4 + m)
                    for w in range(2):
                        n = 2 * m + w
                        for k in range(DC):
                            mm = pe.matmul(PS[:, 1, w * 256:(w + 1) * 256], HT[:, k, n * P:(n + 1) * P],
                                           wz[:, k * 2 * DK:(k + 1) * 2 * DK], start=(k == 0), stop=(k == DC - 1))
                    mm.then_inc(s["zz"], 1)

                def turn(src, hv, b0):
                    for n in range(TILES):
                        mm = pe.transpose(PS[:, b0 + n // 4, (n % 4) * P:(n % 4 + 1) * P],
                                          src[:, hv, n, :, :].rearrange("p w s -> p (w s)"), C("ident"))
                    return mm

                def apply(lhs, rhs, hv):
                    for n in range(TILES):
                        mm = pe.matmul(PS[:, own(hv) + n // 4, (n % 4) * P:(n % 4 + 1) * P], lhs[:, hv, n, :], rhs[:, hv, n, :],
                                       start=True, stop=True)
                    return mm

                def each_batch(hv, lhs, rhs, first):
                    for n in range(TILES):
                        o = PS[:, 4 + hv, n * S:(n + 1) * S]
                        if n == 0 and first:
                            mm = pe.matmul(o, lhs[:, hv, n, :], rhs[:, hv, n, :], start=True, stop=True)
                            continue
                        for b in range(2):
                            r = slice(64 * b, 64 * b + S)
                            mm = pe.matmul(o[r, :], lhs[r, hv, n, r], rhs[r, hv, n, :], start=True, stop=True)
                    return mm

                def norms(h):
                    pe.wait_ge(s["sq"], h * 2 + 2)
                    for c in range(2):
                        for n in range(TILES):
                            mm = pe.matmul(PS[:, 3, c * TILES + n:c * TILES + n + 1], sq[:, c, n * P:(n + 1) * P], C("ones"),
                                           start=True, stop=True)
                    mm.then_inc(s["ss"], 1)

                def decay_sums(h):
                    for hv in range(2):
                        pe.wait_ge(s["gm"], h * 2 + hv + 1)
                        pe.matmul(PS[:, 4 + hv, :], C("cumsum"), flat(gm[:, hv, :, :]), start=True, stop=True).then_inc(s["dps"], 1)

                def scores(h):
                    for c in range(2):
                        pe.wait_ge(s["y"], h * NQ + 2 * c + 2)
                        pe.wait_ge(s["e"], h * 2 + c + 1)
                        for n in range(TILES):
                            for b in range(2):
                                o = n * P + b * S
                                mm = pe.matmul(PS[64 * b:64 * b + S, 4 + c, n * S:(n + 1) * S], y[:, c, o:o + S], y[:, 0, o:o + S],
                                               start=True, stop=True)
                        mm.then_inc(s["kk"], 1)

                def turn_A(h, hv):
                    if hv == 0:
                        pe.wait_ge(s["pd"], h * 2 + 2)
                    else:
                        pe.wait_ge(s["ats"], h * 4 + 2)
                    turn(A, hv, 4).then_inc(s["at"], 1)

                def turn_Pd(h, hv):
                    if hv == 0:
                        pe.wait_ge(s["ats"], h * 4 + 4)
                    else:
                        pe.wait_ge(s["pts"], h * 4 + 2)
                    turn(Pd, hv, 4).then_inc(s["pt"], 1)

                def turn_v(h, hv):
                    pe.wait_ge(s["y"], h * NQ + 6 + 2 * hv)
                    if hv == 0:
                        pe.wait_ge(s["conv"], h * 24 + 24)
                    else:
                        pe.wait_ge(s["vc"], h * 2 + 1)
                    for n in range(TILES):
                        mm = pe.transpose(PS[:, n // 4, (n % 4) * P:(n % 4 + 1) * P], y[:, 2 + hv, n * P:(n + 1) * P], C("ident"))
                    mm.then_inc(s["vt"], 1)

                def project_out(j, b):
                    if b == 0:
                        pe.wait_ge(s["ogs"], j * 2 + 2)
                        pe.wait_ge(s["wof"], j + 1)
                    for w in range(2):
                        n = 2 * b + w
                        for hv in range(2):
                            mm = pe.matmul(PS[:, own(b // 2) + b % 2, w * D:(w + 1) * D], sq[:, hv, n * P:(n + 1) * P], wo[:, hv, :],
                                           start=(hv == 0), stop=(hv == 1))
                    if b % 2:
                        mm.then_inc(s["wo"], 1)

                def chain(j, beside):
                    for k in range(1, LEVELS):
                        for hv in range(2):
                            if k == 1:
                                pe.wait_ge(s["ti"], j * 4 + hv + 3)
                                pe.wait_ge(s["xa"], j * 2 + hv + 1)
                                pe.wait_ge(s["pts"], j * 4 + 4)
                            else:
                                pe.wait_ge(s["tu"], j * 10 + (k - 2) * 2 + hv + 1)
                            turn(T, hv, own(hv)).then_inc(s["tt"], 1)
                            each_batch(hv, AT, T[:, :, :, 0, :], False).then_inc(s["x"], 1)
                        if beside:
                            project(j + 1, k - 1)
                        for hv in range(2):
                            pe.wait_ge(s["xs"], j * 10 + (k - 1) * 2 + hv + 1)
                            pe.wait_ge(s["tts"], j * 24 + (k - 1) * 4 + hv * 2 + 2)
                            each_batch(hv, TT, Xs, True).then_inc(s["yy"], 1)
                        if k < TOP:
                            project_z(j, k - 1)
                        elif beside:
                            project(j + 1, 5)
                    if beside:
                        norms(j + 1)
                    for hv in range(2):
                        pe.wait_ge(s["tu"], j * 10 + 8 + hv + 1)
                        if beside and hv == 1:
                            pe.wait_ge(s["nm"], j + 2)
                        turn(T, hv, own(hv)).then_inc(s["tt"], 1)
                    if beside:
                        decay_sums(j + 1)
                    for hv in range(2):
                        pe.wait_ge(s["tts"], j * 24 + 20 + hv * 2 + 2)
                        pe.wait_ge(s["vs"], j * 2 + hv + 1)
                        apply(TT, V, hv).then_inc(s["dl"], 1)
                    if beside:
                        project(j + 1, 6)
                    for hv in range(2):
                        pe.wait_ge(s["ds"], j * 2 + hv + 1)
                        apply(PT, dl, hv).then_inc(s["u"], 1)
                    if beside:
                        scores(j + 1)
                        project(j + 1, 7)
                    for hv in range(2):
                        pe.wait_ge(s[f"og{hv}"], j + 1)
                        for n in range(TILES):
                            mm = pe.transpose(PS[:, own(hv) + n // 4, (n % 4) * P:(n % 4 + 1) * P], dl[:, hv, n, :], C("ident"))
                        mm.then_inc(s["ogt"], 1)
                    project_out(j, 0)
                    if beside:
                        turn_A(j + 1, 0)
                    project_out(j, 1)
                    if beside:
                        turn_A(j + 1, 1)
                    project_out(j, 2)
                    if beside:
                        turn_Pd(j + 1, 0)
                    project_out(j, 3)
                    if beside:
                        turn_v(j + 1, 0)
                        turn_Pd(j + 1, 1)
                        turn_v(j + 1, 1)

                for q in range(NQ):
                    project(0, q)
                norms(0)
                decay_sums(0)
                scores(0)
                turn_A(0, 0)
                turn_A(0, 1)
                turn_Pd(0, 0)
                turn_v(0, 0)
                turn_Pd(0, 1)
                turn_v(0, 1)
                pe.wait_ge(s["zero"], 3)
                with pe.Fori(0, LAST) as j:
                    chain(j, True)
                chain(LAST, False)

            @block.scalar
            def _(a):
                def tap(h, q):
                    c, f = q // 2, slot(h, q)
                    if q == 0:
                        a.wait_ge(s["cin"], h * 16 + 16)
                    a.wait_ge(s["pj"], h * NQ + q + 1)
                    if isinstance(h, int):
                        if q >= 2:
                            a.wait_ge(s["y"], q - 1)
                    elif q == 0 or q >= 5:
                        a.wait_ge(s["y"], h * NQ + q - 1 if q != 5 else h * NQ)
                    else:
                        a.wait_ge(s["y"], h * NQ + q)
                    a.activation(acc[:, f, :], PS[:, f, :], ACT.Copy, scale=wc[:, 4 * c + 3:4 * c + 4]).then_inc(s["tap"], 1)

                def tanh(h, q):
                    a.wait_ge(s["conv"], h * 24 + q * 3 + 3)
                    a.activation(th[:, slot(h, q), :], acc[:, slot(h, q), :], ACT.Tanh, scale=0.5).then_inc(s["th"], 1)

                def tanh_z(j, m):
                    a.wait_ge(s["zz"], j * 4 + m + 1)
                    if m == 0:
                        a.wait_ge(s["y"], j * NQ + NQ)
                    a.activation(th[:, 1, :], PS[:, 1, :], ACT.Tanh, scale=0.5).then_inc(s["zt"], 1)

                def split(dst, hv, b0, done):
                    for b in range(2):
                        a.activation(blocks(dst[:, hv, :, :], b),
                                     blocks(wide(b0).rearrange("p (n t) -> p n t", t=P), b), ACT.Copy).then_inc(done, 1)

                def square(h, c):
                    a.wait_ge(s["y"], h * NQ + 2 * c + 2)
                    a.activation(sq[:, c, :], y[:, c, :], ACT.Square).then_inc(s["sq"], 1)

                def decays(h):
                    for hv in range(2):
                        a.wait_ge(s["dps"], h * 2 + hv + 1)
                        a.activation(E[:, hv, :, :], bank(4 + hv), ACT.Exp).then_inc(s["e"], 1)

                def keep_A(h, hv):
                    a.wait_ge(s["at"], h * 2 + hv + 1)
                    split(AT, hv, 4, s["ats"])

                def keep_Pd(h, hv):
                    a.wait_ge(s["pt"], h * 2 + hv + 1)
                    split(PT, hv, 4, s["pts"])

                def keep_v(h, hv):
                    a.wait_ge(s["vt"], h * 2 + hv + 1)
                    a.activation(flat(V[:, hv, :, :]), wide(0), ACT.Copy).then_inc(s["vc"], 1)

                def prepare(h, beside):
                    keep_A(h, 0)
                    keep_A(h, 1)
                    keep_Pd(h, 0)
                    if beside:
                        tanh(h, 7)
                    keep_v(h, 0)
                    keep_Pd(h, 1)
                    keep_v(h, 1)

                def chain(j, beside):
                    for k in range(1, LEVELS):
                        for hv in range(2):
                            a.wait_ge(s["tt"], j * 12 + (k - 1) * 2 + hv + 1)
                            split(TT, hv, own(hv), s["tts"])
                        if beside:
                            tap(j + 1, k - 1)
                            if k == 3:
                                square(j + 1, 0)
                            if k == TOP:
                                square(j + 1, 1)
                            tanh(j + 1, k - 1)
                        if k < TOP:
                            tanh_z(j, k - 1)
                        elif beside:
                            tap(j + 1, 5)
                    for hv in range(2):
                        a.wait_ge(s["tt"], j * 12 + 10 + hv + 1)
                        split(TT, hv, own(hv), s["tts"])
                    if beside:
                        decays(j + 1)
                        tanh(j + 1, 5)
                    for hv in range(2):
                        a.wait_ge(s["dl"], j * 2 + hv + 1)
                        a.activation(flat(dl[:, hv, :, :]), wide(own(hv)), ACT.Copy).then_inc(s["ds"], 1)
                    if beside:
                        tap(j + 1, 6)
                    for hv in range(2):
                        a.wait_ge(s["u"], j * 2 + hv + 1)
                        a.activation(sq[:, hv, :], wide(own(hv)), ACT.Square).then_inc(s["us"], 1)
                    if beside:
                        tanh(j + 1, 6)
                        tap(j + 1, 7)
                    for hv in range(2):
                        a.wait_ge(s["ogt"], j * 2 + hv + 1)
                        a.activation(sq[:, hv, :], wide(own(hv)), ACT.Copy).then_inc(s["ogs"], 1)
                    if beside:
                        prepare(j + 1, True)

                for q in range(NQ):
                    tap(0, q)
                    if q > 0:
                        tanh(0, q - 1)
                tanh(0, NQ - 1)
                square(0, 0)
                square(0, 1)
                decays(0)
                a.wait_ge(s["zero"], 3)
                prepare(0, False)
                with a.Fori(0, LAST) as j:
                    chain(j, True)
                chain(LAST, False)

            @block.gpsimd
            def _(g):
                for m in (AT, TT, PT):
                    g.memset(m[:, :, :, :], 0.0).then_inc(s["zero"], 1)

                def decays(h):
                    for hv in range(2):
                        g.wait_ge(s["gj"], h * 2 + 2)
                        g.tensor_tensor(gm[:, hv, :, :], over(C("strict"), TILES), each(gj[:, :, hv], S), ALU.mult).then_inc(s["gm"], 1)

                def factors(h):
                    g.wait_ge(s["nm"], h + 1)
                    g.tensor_tensor(rr[:, :], nm[:, :], C("mhalf")[:, 0:2 * TILES], ALU.pow).then_inc(s["rr"], 1)
                    g.wait_ge(s["rr"], h * 5 + 1)
                    for hv in range(2):
                        g.tensor_tensor(bk[:, hv, :], gj[:, :, 2 + hv], rr[:, 0:TILES], ALU.mult).then_inc(s["rr"], 1)
                    for hv in range(2):
                        g.wait_ge(s["rr"], h * 5 + 2 + hv)
                        g.tensor_tensor(dd[:, hv, :], bk[:, hv, :], rr[:, 0:TILES], ALU.mult).then_inc(s["rr"], 1)
                    for hv in range(2):
                        g.wait_ge(s["rr"], h * 5 + 4 + hv)
                        g.wait_ge(s["e"], h * 2 + hv + 1)
                        g.tensor_tensor(Xs[:, hv, :, :], E[:, hv, :, :], each(dd[:, hv, :], S), ALU.mult).then_inc(s["ed"], 1)
                    for hv in range(2):
                        g.wait_ge(s["e"], h * 2 + hv + 1)
                        g.tensor_tensor(Et[:, hv, :, :], E[:, hv, :, :], over(C("tril"), TILES), ALU.mult).then_inc(s["et"], 1)

                def first_T(h):
                    for hv in range(2):
                        g.wait_ge(s["av"], h * 2 + hv + 1)
                        g.tensor_tensor(Xs[:, hv, :, :], A[:, hv, :, 0, :], over(C("lvl0"), TILES), ALU.mult).then_inc(s["ti"], 1)
                    for hv in range(2):
                        g.wait_ge(s["ti"], h * 4 + hv + 1)
                        g.tensor_tensor(T[:, hv, :, :, :], C("eye").unsqueeze(1).unsqueeze(1).broadcast_to([P, TILES, 2, S]),
                                        twice(Xs[:, hv, :, :]), ALU.subtract).then_inc(s["ti"], 1)

                def scale_v(h):
                    for hv in range(2):
                        g.wait_ge(s["vc"], h * 2 + hv + 1)
                        g.tensor_tensor(V[:, hv, :, :], V[:, hv, :, :], each(bk[:, hv, :], DK), ALU.mult).then_inc(s["vs"], 1)

                def chain(j, beside):
                    if beside:
                        decays(j + 1)
                        factors(j + 1)
                    for hv in range(2):
                        g.wait_ge(s["ms"], j * 6 + hv * 3 + 3)
                        g.tensor_tensor(ms[:, hv, :], ms[:, hv, :], C("mhalf")[:, 0:TILES], ALU.pow).then_inc(s["fz"], 1)
                        g.wait_ge(s["fz"], j * 4 + hv * 2 + 1)
                        g.tensor_tensor(ms[:, hv, :], ms[:, hv, :], rq[:, 0, :], ALU.mult).then_inc(s["fz"], 1)
                    g.wait_ge(s["fz"], j * 4 + 4)
                    g.wait_ge(s["gz"], j * 2 + 2)
                    g.tensor_tensor(dl[:, 1, :, :], dl[:, 1, :, :], each(ms[:, 1, :], DK), ALU.mult).then_inc(s["og1"], 1)
                    if beside:
                        first_T(j + 1)
                        scale_v(j + 1)

                decays(0)
                factors(0)
                first_T(0)
                scale_v(0)
                with g.Fori(0, LAST) as j:
                    chain(j, True)
                chain(LAST, False)

            @block.vector
            def _(v):
                def pick(h):
                    v.tensor_copy(gj[:, :, 0:2], ga[:, :, bass.ds(h * 2, 2)]).then_inc(s["gj"], 1)
                    v.tensor_copy(gj[:, :, 2:4], ga[:, :, bass.ds(h * 2 + HV, 2)]).then_inc(s["gj"], 1)

                def conv(h, q):
                    c, f = q // 2, slot(h, q)
                    for k in range(3):
                        sh = k + 1
                        a0 = acc[:, f, :].rearrange("p (b s) -> p b s", s=S)[:, :, sh:S]
                        p0 = PS[:, f, :].rearrange("p (b s) -> p b s", s=S)[:, :, 0:S - sh]
                        if k == 0:
                            v.wait_ge(s["tap"], h * NQ + q + 1)
                        else:
                            v.wait_ge(s["conv"], h * 24 + q * 3 + k)
                        v.scalar_tensor_tensor(a0, p0, wc[:, 4 * c + 2 - k:4 * c + 3 - k], a0, ALU.mult, ALU.add).then_inc(s["conv"], 1)

                def silu(h, q):
                    c, f = q // 2, q % 2
                    v.wait_ge(s["th"], h * NQ + q + 1)
                    v.scalar_tensor_tensor(y[:, c, f * 512:(f + 1) * 512], th[:, slot(h, q), :], 1.0, acc[:, slot(h, q), :],
                                           ALU.add, ALU.mult).then_inc(s["y"], 1)

                def silu_z(j, m):
                    v.wait_ge(s["zt"], j * 4 + m + 1)
                    v.scalar_tensor_tensor(z2[:, 2 * m:2 * m + 2, :, :].rearrange("p n h c -> p (n h c)"), th[:, 1, :], 1.0,
                                           PS[:, 1, :], ALU.add, ALU.mult).then_inc(s["z2"], 1)

                def norms(h):
                    v.wait_ge(s["ss"], h + 1)
                    v.tensor_scalar(nm[:, :], PS[:, 3, 0:2 * TILES], 4e-12, None, ALU.max).then_inc(s["nm"], 1)

                def make_A(h):
                    for hv in range(2):
                        v.wait_ge(s["ed"], h * 2 + hv + 1)
                        v.wait_ge(s["kk"], h * 2 + 1)
                        v.tensor_tensor(A[:, hv, :, :, :], twice(bank(4)), twice(Xs[:, hv, :, :]), ALU.mult).then_inc(s["av"], 1)
                    for hv in range(2):
                        v.wait_ge(s["et"], h * 2 + hv + 1)
                        v.wait_ge(s["kk"], h * 2 + 2)
                        v.tensor_tensor(Pd[:, hv, :, :, :], twice(bank(5)), twice(Et[:, hv, :, :]), ALU.mult).then_inc(s["pd"], 1)

                def chain(j, beside):
                    v.wait_ge(s["rr"], j * 5 + 1)
                    v.tensor_copy(rq[:, 0, :], rr[:, TILES:2 * TILES]).then_inc(s["rq"], 1)
                    v.tensor_tensor(rq[:, 1, :], rr[:, TILES:2 * TILES], rr[:, TILES:2 * TILES], ALU.mult).then_inc(s["rq"], 1)
                    v.wait_ge(s["oin"], j * 16 + 16)
                    v.tensor_scalar(wo[:, :, :], wo[:, :, :], nw[:, :], DK ** -0.5 / 4, ALU.mult, ALU.mult).then_inc(s["wof"], 1)
                    for k in range(1, LEVELS):
                        for hv in range(2):
                            v.wait_ge(s["x"], j * 10 + (k - 1) * 2 + hv + 1)
                            v.tensor_tensor(Xs[:, hv, :, :], bank(4 + hv), over(C(f"lvl{k}"), TILES), ALU.mult).then_inc(s["xs"], 1)
                        if beside:
                            if k == 1:
                                pick(j + 1)
                            conv(j + 1, k - 1)
                        for hv in range(2):
                            v.wait_ge(s["yy"], j * 10 + (k - 1) * 2 + hv + 1)
                            v.tensor_tensor(T[:, hv, :, :, :], T[:, hv, :, :, :], twice(bank(4 + hv)), ALU.subtract).then_inc(s["tu"], 1)
                        if beside:
                            silu(j + 1, k - 1)
                        if k < TOP:
                            silu_z(j, k - 1)
                    if beside:
                        norms(j + 1)
                        conv(j + 1, 5)
                        silu(j + 1, 5)
                        conv(j + 1, 6)
                    for hv in range(2):
                        v.wait_ge(s["us"], j * 2 + hv + 1)
                        v.tensor_reduce(ms[:, hv, :], sq[:, hv, :].rearrange("p (n c) -> p n c", c=DK), AX.X, ALU.add).then_inc(s["ms"], 1)
                        v.wait_ge(s["ms"], j * 6 + hv * 3 + 1)
                        v.wait_ge(s["rq"], j * 2 + 2)
                        v.tensor_tensor(ms[:, hv, :], ms[:, hv, :], rq[:, 1, :], ALU.mult).then_inc(s["ms"], 1)
                        v.wait_ge(s["ms"], j * 6 + hv * 3 + 2)
                        v.tensor_scalar(ms[:, hv, :], ms[:, hv, :], 1.0 / (4 * DK * DK), 1e-6, ALU.mult, ALU.add).then_inc(s["ms"], 1)
                        v.tensor_tensor(dl[:, hv, :, :], wide(own(hv)).rearrange("p (n c) -> p n c", c=DK),
                                        z2[:, :, hv, :], ALU.mult).then_inc(s["gz"], 1)
                    v.wait_ge(s["fz"], j * 4 + 2)
                    v.tensor_tensor(dl[:, 0, :, :], dl[:, 0, :, :], each(ms[:, 0, :], DK), ALU.mult).then_inc(s["og0"], 1)
                    if beside:
                        silu(j + 1, 6)
                        make_A(j + 1)
                        conv(j + 1, 7)
                    for m in range(2):
                        if beside and m == 1:
                            silu(j + 1, 7)
                        v.wait_ge(s["wo"], j * 2 + m + 1)
                        v.tensor_tensor(X[:, 4 * m:4 * m + 4, :], X[:, 4 * m:4 * m + 4, :],
                                        PS[:, own(m):own(m) + 2, :].rearrange("p k (w c) -> p (k w) c", w=2), ALU.add).then_inc(s["xa"], 1)

                v.sem_inc(s["xa"], 1)
                v.sem_inc(s["xa"], 1)
                v.wait_ge(s["nin"], 16)
                pick(0)
                for q in range(NQ):
                    conv(0, q)
                    if q > 0:
                        silu(0, q - 1)
                silu(0, NQ - 1)
                norms(0)
                make_A(0)
                with v.Fori(0, LAST) as j:
                    chain(j, True)
                chain(LAST, False)


def phase4(nc, d, sb, semaphores, C, over, each, X, PS, carrier, norm_stats, norm_root, norm_apply, norm_turn, hT_psum):
    W = NE * EI
    with ExitStack() as ctx:
        wr = sb(ctx, "w_router", [P, DC, NE])
        wg = sb(ctx, "wg", [P, DC, W])
        wu = sb(ctx, "wu", [P, DC, W])
        wd = sb(ctx, "wd", [P, MC, D])
        hT = sb(ctx, "hT4", [P, 2, DC, P])
        th = sb(ctx, "th4", [P, 2, 2, 512])
        act = sb(ctx, "act", [P, 2, W])
        acT = sb(ctx, "acT", [P, 2, W])
        lg = sb(ctx, "lg", [P, 2, NE])
        lm = sb(ctx, "lm", [P, 2, 1])
        top = sb(ctx, "top", [P, 2, TOPK])
        rep = sb(ctx, "rep", [P, 2, NE])
        rw = sb(ctx, "rw", [P, 2, NE])
        names = "stats root turned hT lgt le rt gu th y ht aT dn res"
        s = semaphores(ctx, "wsm wdn " + "".join(f"wup{m} " for m in range(MB)) + " ".join(f"{n}{p}" for n in names.split() for p in range(2)), "p4_")
        with nc.Block() as block:
            @block.sync
            def _(sp):
                sp.dma_start(wr[:, :, :], d["moe_gate"]).then_inc(s["wsm"], 16)
                for m in range(MB):
                    b = slice(m * 512, (m + 1) * 512)
                    sp.dma_start(wg[:, :, b], d["moe_g"][:, :, b]).then_inc(s[f"wup{m}"], 16)
                    sp.dma_start(wu[:, :, b], d["moe_u"][:, :, b]).then_inc(s[f"wup{m}"], 16)
                sp.dma_start(wd[:, :, :], d["moe_d"]).then_inc(s["wdn"], 16)

            @block.tensor
            def _(pe):
                for p in range(2):
                    pe.sem_inc(s[f"turned{p}"], 1)
                pe.wait_ge(s["wsm"], 16)
                with pe.Fori(0, TILES // 2) as i:
                    for p in range(2):
                        pe.wait_ge(s[f"res{p}"], i + 1)
                        norm_turn(pe, i, p, 4 * p, s[f"stats{p}"], s[f"turned{p}"])
                    for p in range(2):
                        pe.wait_ge(s[f"hT{p}"], i + 1)
                        for k in range(DC):
                            mm = pe.matmul(PS[:, 4 * p + 3, 0:NE], hT[:, p, k, :], wr[:, k, :], start=(k == 0), stop=(k == DC - 1))
                        mm.then_inc(s[f"lgt{p}"], 1)
                    for p in range(2):
                        pe.wait_ge(s[f"rt{p}"], i * 6 + 2)
                        for m in range(MB):
                            pe.wait_ge(s[f"wup{m}"], 32)
                            pe.wait_ge(s[f"y{p}"], i * (2 * MB + 1) + 2 * m + 2)
                            for w, o in ((wg, 0), (wu, 1)):
                                for k in range(DC):
                                    mm = pe.matmul(PS[:, 4 * p + 2 * (m % 2) + o, :], hT[:, p, k, :], w[:, k, m * 512:(m + 1) * 512],
                                                   start=(k == 0), stop=(k == DC - 1))
                            mm.then_inc(s[f"gu{p}"], 1)
                    pe.wait_ge(s["wdn"], 16)
                    for p in range(2):
                        pe.wait_ge(s[f"y{p}"], (i + 1) * (2 * MB + 1) + 4)
                        for m in range(MB + 1):
                            if m < MB:
                                pe.wait_ge(s[f"aT{p}"], i * MB + m + 1)
                                for q in range(4):
                                    c = m * 4 + q
                                    mm = pe.transpose(PS[:, 4 * p + m % 2, q * P:(q + 1) * P], act[:, p, c * P:(c + 1) * P], C("ident"))
                                mm.then_inc(s[f"ht{p}"], 1)
                            if m > 0:
                                pe.wait_ge(s[f"aT{p}"], i * MB + m + 2)
                                for q in range(4):
                                    c = (m - 1) * 4 + q
                                    mm = pe.matmul(PS[:, 4 * p + 2, 0:D], acT[:, p, c * P:(c + 1) * P], wd[:, c, :],
                                                   start=(c == 0), stop=(c == MC - 1))
                        mm.then_inc(s[f"dn{p}"], 1)

            @block.scalar
            def _(a):
                for p in range(2):
                    a.sem_inc(s[f"aT{p}"], 2)
                with a.Fori(0, TILES // 2) as i:
                    for p in range(2):
                        a.wait_ge(s[f"turned{p}"], i + 2)
                        a.activation(hT[:, p, :, :], hT_psum(4 * p), ACT.Copy).then_inc(s[f"hT{p}"], 1)
                    for p in range(2):
                        a.wait_ge(s[f"rt{p}"], i * 6 + 2)
                        a.activation(lg[:, p, :], lg[:, p, :], ACT.Exp).then_inc(s[f"le{p}"], 1)
                    for p in range(2):
                        for m in range(MB):
                            a.wait_ge(s[f"gu{p}"], i * MB + m + 1)
                            a.activation(th[:, p, m % 2, :], PS[:, 4 * p + 2 * (m % 2), :], ACT.Tanh, scale=0.5).then_inc(s[f"th{p}"], 1)
                    for p in range(2):
                        for m in range(MB):
                            a.wait_ge(s[f"ht{p}"], i * MB + m + 1)
                            a.activation(acT[:, p, m * 512:(m + 1) * 512], PS[:, 4 * p + m % 2, :], ACT.Copy).then_inc(s[f"aT{p}"], 1)

            @block.gpsimd
            def _(g):
                with g.Fori(0, TILES // 2) as i:
                    for p in range(2):
                        norm_root(g, i, p, s[f"stats{p}"], s[f"root{p}"])

            @block.vector
            def _(v):
                for p in range(2):
                    v.sem_inc(s[f"res{p}"], 1)
                    v.sem_inc(s[f"y{p}"], 4)
                with v.Fori(0, TILES // 2) as i:
                    for p in range(2):
                        norm_stats(v, i, p, s[f"stats{p}"], i)
                    for p in range(2):
                        norm_apply(v, i, p, s[f"stats{p}"], s[f"root{p}"], s[f"turned{p}"], i)
                    for p in range(2):
                        rt = s[f"rt{p}"]
                        v.wait_ge(s[f"lgt{p}"], i + 1)
                        v.tensor_reduce(lm[:, p, :], PS[:, 4 * p + 3, 0:NE], AX.X, ALU.max).then_inc(rt, 1)
                        v.wait_ge(rt, i * 6 + 1)
                        v.tensor_scalar(lg[:, p, :], PS[:, 4 * p + 3, 0:NE], lm[:, p, :], None, ALU.subtract).then_inc(rt, 1)
                    for p in range(2):
                        rt = s[f"rt{p}"]
                        v.wait_ge(s[f"le{p}"], i + 1)
                        v.memset(carrier[:, :], 0.0)
                        v.max(top[:, p, :], lg[:, p, :]).then_inc(rt, 1)
                        v.wait_ge(rt, i * 6 + 3)
                        v.memset(carrier[:, :], 0.0)
                        v.match_replace(rep[:, p, :], top[:, p, :], lg[:, p, :], -1.0).then_inc(rt, 1)
                        v.tensor_reduce(lm[:, p, :], top[:, p, :], AX.X, ALU.add).then_inc(rt, 1)
                        v.wait_ge(rt, i * 6 + 4)
                        v.scalar_tensor_tensor(rw[:, p, :], rep[:, p, :], 0.0, lg[:, p, :], ALU.is_lt, ALU.mult)
                        v.wait_ge(rt, i * 6 + 5)
                        v.reciprocal(lm[:, p, :], lm[:, p, :]).then_inc(rt, 1)
                        v.wait_ge(rt, i * 6 + 6)
                        v.tensor_scalar(rw[:, p, :], rw[:, p, :], lm[:, p, :], 0.5, ALU.mult, ALU.mult)
                    for p in range(2):
                        yy = s[f"y{p}"]
                        y0 = i * (2 * MB + 1) + 4
                        for m in range(MB):
                            out = act[:, p, m * 512:(m + 1) * 512]
                            v.wait_ge(s[f"th{p}"], i * MB + m + 1)
                            v.scalar_tensor_tensor(out, th[:, p, m % 2, :], 1.0, PS[:, 4 * p + 2 * (m % 2), :], ALU.add, ALU.mult).then_inc(yy, 1)
                            v.wait_ge(yy, y0 + 2 * m + 1)
                            v.tensor_tensor(out, out, PS[:, 4 * p + 2 * (m % 2) + 1, :], ALU.mult).then_inc(yy, 1)
                        v.wait_ge(yy, y0 + 2 * MB)
                        x = act[:, p, :].rearrange("p (e i) -> p e i", i=EI)
                        v.tensor_tensor(x, x, each(rw[:, p, :], EI), ALU.mult).then_inc(yy, 1)
                    for p in range(2):
                        v.wait_ge(s[f"dn{p}"], i + 1)
                        t = bass.ds(i * 2 + p, 1)
                        v.tensor_tensor(X[:, t, :], X[:, t, :], PS[:, 4 * p + 2, 0:D].unsqueeze(1), ALU.add).then_inc(s[f"res{p}"], 1)




def layouts(i):
    def T(a):
        return np.ascontiguousarray(a)
    g = {k: np.asarray(v) for k, v in i.items()}
    n = {"consts": CONSTS, "x": g["x"]}
    ctx = g["ctx_512"]
    rolled = np.concatenate([ctx[..., DCTX // 2:], ctx[..., :DCTX // 2]], axis=-1)
    n["ctx"], n["ctx_rolled"] = T(ctx.transpose(1, 0, 2)), T(rolled.transpose(1, 0, 2))
    n["ctxT"], n["ctxT_rolled"] = T(ctx.transpose(2, 0, 1)), T(rolled.transpose(2, 0, 1))
    n["l0x_k"] = np.concatenate([g["L0_xattn_Wq"].reshape(H0, K0, D), g["L0_xattn_w_kc_q"], g["L0_xattn_w_kc_kv"],
                                 g["L0_xattn_Wo"].T.reshape(H0, K0, D)], axis=2)
    n["l0x_r"] = np.concatenate([g["L0_xattn_W_qr"].transpose(0, 2, 1), g["L0_xattn_W_kr"].transpose(0, 2, 1)], axis=2)

    def chunks(a):
        return T(a.reshape(-1, P, a.shape[1]).transpose(1, 0, 2))

    n["attn_w"] = np.concatenate([chunks(g["L0_attn_" + w]) for w in ("Wq", "Wk", "Wv", "Wo")], axis=2)
    n["xattn_w"] = np.concatenate([chunks(T(g["L1_xattn_Wq"].T)), chunks(T(g["L1_xattn_Wout"].T))], axis=2)
    n["xattn_kv"] = T(g["L1_xattn_Wkv_expand"].T)
    n["ffn_ug"] = chunks(T(np.concatenate([g["L0_ffn_W_up"], g["L0_ffn_W_gate"]], axis=0).T))
    n["ffn_ws"] = g["L0_ffn_Wscale_ug"].reshape(1, -1)
    n["ffn_dn"] = chunks(T(g["L0_ffn_W_down"].T))
    n["ffn_wsd"] = g["L0_ffn_Wscale_dp"].reshape(1, -1)
    n["ffn_su"] = T(g["L0_ffn_SU_ug"].reshape(DC, P).T)
    n["ffn_sud"] = T(g["L0_ffn_SU_dp"].reshape(IC, P).T)
    wqkv = chunks(T(g["L1_attn_W_qkv"].T))
    wz = chunks(T(g["L1_attn_W_z"].T))
    cw = g["L1_attn_conv_w"].reshape(-1, P, 4)
    wo = chunks(T(g["L1_attn_W_out"].T))
    packs = []
    for j in range(HK):
        blocks = (HK + j, j, 2 * HK + 2 * j, 2 * HK + 2 * j + 1)
        packs.append(np.concatenate(
            [np.concatenate([wqkv[:, :, b * P:(b + 1) * P] for b in blocks], axis=2).reshape(P, -1),
             wz[:, :, j * 2 * DK:(j + 1) * 2 * DK].reshape(P, -1),
             wo[:, 2 * j:2 * j + 2, :].reshape(P, -1)] + [cw[b] for b in blocks], axis=1))
    n["gdn_w"] = np.stack(packs)
    n["gdn_ab"] = chunks(T(np.concatenate([g["L1_attn_W_a"], g["L1_attn_W_b"]], axis=0).T))
    n["gdn_al"], n["gdn_dt"] = g["L1_attn_A_log"].reshape(1, -1), g["L1_attn_dt_bias"].reshape(1, -1)
    n["gdn_nw"] = g["L1_attn_norm_w"].reshape(-1, 1)
    n["moe_gate"] = chunks(T(g["L1_ffn_gate_w"].T))
    n["moe_g"] = chunks(T(g["L1_ffn_Wg"].reshape(-1, D).T))
    n["moe_u"] = chunks(T(g["L1_ffn_Wu"].reshape(-1, D).T))
    n["moe_d"] = chunks(T(g["L1_ffn_Wd"].transpose(0, 2, 1).reshape(-1, D)))
    return {k: T(v) for k, v in n.items()}




def kernel(**inputs):
    import concourse.bacc as _bacc
    from concourse.bass_utils import run_bass_kernel_spmd as _run

    nc = _bacc.Bacc("TRN2", target_bir_lowering=False, num_devices=1)
    arrays, args = {}, {}
    for name, a in layouts(inputs).items():
        arrays[f"in_{name}"] = a
        args[name] = nc.dram_tensor(f"in_{name}", a.shape, mybir.dt.from_np(a.dtype), kind="ExternalInput").ap()
    out = nc.dram_tensor("out_x", (B, S, D), F32, kind="ExternalOutput").ap()
    build(nc, args, out)
    r = _run(nc, [arrays], core_ids=[0])
    return r.results[0]["out_x"]
```
